# Optimizing a Trainium2 kernel written in Bass

```python
import numpy as np
import jax
import jax.numpy as jnp

def _softmax(x, axis=-1):
    return jax.nn.softmax(x, axis=axis)

def _gelu(x):
    return jax.nn.gelu(x, approximate=True)

def _silu(x):
    return jax.nn.silu(x)

def _sigmoid(x):
    return jax.nn.sigmoid(x)

def _layernorm(x, axis=-1, eps=1e-05):
    m = jnp.mean(x, axis=axis, keepdims=True)
    v = jnp.var(x, axis=axis, keepdims=True)
    return (x - m) / jnp.sqrt(v + eps)

def _scatter_add(tgt, idx, src, axis=0):
    return tgt.at[idx].add(src)

def _segment_sum(src, seg, n):
    return jax.ops.segment_sum(src, seg, n)
kernel_name = 'mk_gnn_resnorm_d2_gnn_r16_06e600'

def setup_inputs(seed: int=0):
    np.random.seed(seed)
    _w = jnp.asarray

    def _rec_inputs():
        import jax
        import jax.numpy as jnp
        _gk = jax.random.key(seed)
        x = -0.000202 + 1 * jax.random.normal(jax.random.fold_in(_gk, 1), (3125, 128), jnp.float32)
        src = jax.random.randint(jax.random.fold_in(_gk, 2), (100000,), 0, 3125, jnp.int32)
        dst = jax.random.randint(jax.random.fold_in(_gk, 3), (100000,), 0, 3125, jnp.int32)
        _o = jnp.argsort(dst, stable=True)
        src = src[_o]
        dst = dst[_o]
        return (x, src, dst)
    x, src, dst = _rec_inputs()

    def _L0_gnn_setup():
        import jax, jax.numpy as jnp
        import numpy as np
        N_NODES = 3125
        N_EDGES = 50000
        IN_FEATS = 128
        H_FEATS = 128

        def _sage_conv(x, src, dst, W_neigh, W_self, b):
            msg = x[src]
            summed = jax.ops.segment_sum(msg, dst, num_segments=N_NODES)
            deg = jax.ops.segment_sum(jnp.ones((src.shape[0],), x.dtype), dst, num_segments=N_NODES)
            mean = summed / jnp.maximum(deg, 1.0)[:, None]
            return x @ W_self + mean @ W_neigh + b
        key = jax.random.key(seed)
        ks = jax.random.split(key, 8)
        x = jax.random.normal(ks[0], (N_NODES, IN_FEATS), dtype=jnp.float32)
        src = jax.random.randint(ks[1], (N_EDGES,), 0, N_NODES, dtype=jnp.int32)
        dst = jax.random.randint(ks[2], (N_EDGES,), 0, N_NODES, dtype=jnp.int32)
        s1 = 1.0 / np.sqrt(IN_FEATS)
        s2 = 1.0 / np.sqrt(H_FEATS)
        W_self1 = jax.random.normal(ks[3], (IN_FEATS, H_FEATS), dtype=jnp.float32) * s1
        W_neigh1 = jax.random.normal(ks[4], (IN_FEATS, H_FEATS), dtype=jnp.float32) * s1
        b1 = jnp.zeros((H_FEATS,), dtype=jnp.float32)
        W_self2 = jax.random.normal(ks[5], (H_FEATS, H_FEATS), dtype=jnp.float32) * s2
        W_neigh2 = jax.random.normal(ks[6], (H_FEATS, H_FEATS), dtype=jnp.float32) * s2
        b2 = jnp.zeros((H_FEATS,), dtype=jnp.float32)
        return {'x': x, 'src': src, 'dst': dst, 'W_self1': W_self1, 'W_neigh1': W_neigh1, 'b1': b1, 'W_self2': W_self2, 'W_neigh2': W_neigh2, 'b2': b2}
    _L0_gnn_all = _L0_gnn_setup()
    _L0_gnn_in = {k: v for k, v in _L0_gnn_all.items() if k in ('W_self1', 'W_neigh1', 'b1', 'W_self2', 'W_neigh2', 'b2')}
    del _L0_gnn_all

    def _L1_gnn_setup():
        import jax, jax.numpy as jnp
        import numpy as np
        N, E, F = (3125, 50000, 128)
        EPS_VAR = 1e-05
        EPS_LN = 1e-05

        def _layer_norm(x, w, b):
            m = jnp.mean(x, axis=-1, keepdims=True)
            v = jnp.mean((x - m) ** 2, axis=-1, keepdims=True)
            return (x - m) * jax.lax.rsqrt(v + EPS_LN) * w + b

        def _pna_conv(x, src, dst, deg, avg_log, W_pre, b_pre, W_post, b_post, W_lin, b_lin):
            Fin = x.shape[1]
            xi = x @ W_pre[:Fin]
            xj = x @ W_pre[Fin:]
            h = xi[dst] + xj[src] + b_pre
            degc = jnp.maximum(deg, 1.0)[:, None]
            mean = jax.ops.segment_sum(h, dst, N) / degc
            mean_sq = jax.ops.segment_sum(h * h, dst, N) / degc
            std = jnp.sqrt(jax.nn.relu(mean_sq - mean * mean) + EPS_VAR)
            mx = jax.ops.segment_max(h, dst, N)
            mn = jax.ops.segment_min(h, dst, N)
            has_nbr = (deg > 0)[:, None]
            mx = jnp.where(has_nbr, mx, 0.0)
            mn = jnp.where(has_nbr, mn, 0.0)
            agg = jnp.concatenate([mean, mx, mn, std], axis=-1)
            amp = jnp.log(degc + 1.0) / avg_log
            att = avg_log / jnp.log(degc + 1.0)
            out = jnp.concatenate([agg, agg * amp, agg * att], axis=-1)
            out = jnp.concatenate([x, out], axis=-1) @ W_post + b_post
            return out @ W_lin + b_lin
        key = jax.random.key(seed)
        ks = jax.random.split(key, 32)
        d = {}
        d['x'] = jax.random.normal(ks[0], (N, F), jnp.float32)
        d['edge_index'] = jax.random.randint(ks[1], (2, E), 0, N, dtype=jnp.int32)
        ki = 2
        for l in range(2):
            d[f'W_pre{l}'] = 0.05 * jax.random.normal(ks[ki], (2 * F, F), jnp.float32)
            ki += 1
            d[f'b_pre{l}'] = jnp.zeros((F,), jnp.float32)
            d[f'W_post{l}'] = 0.05 * jax.random.normal(ks[ki], (13 * F, F), jnp.float32)
            ki += 1
            d[f'b_post{l}'] = jnp.zeros((F,), jnp.float32)
            d[f'W_lin{l}'] = 0.05 * jax.random.normal(ks[ki], (F, F), jnp.float32)
            ki += 1
            d[f'b_lin{l}'] = jnp.zeros((F,), jnp.float32)
            d[f'ln_w{l}'] = jnp.ones((F,), jnp.float32)
            d[f'ln_b{l}'] = jnp.zeros((F,), jnp.float32)
        return d
    _L1_gnn_all = _L1_gnn_setup()
    _L1_gnn_in = {k: v for k, v in _L1_gnn_all.items() if k in ('W_pre0', 'b_pre0', 'W_post0', 'b_post0', 'W_lin0', 'b_lin0', 'ln_w0', 'ln_b0', 'W_pre1', 'b_pre1', 'W_post1', 'b_post1', 'W_lin1', 'b_lin1', 'ln_w1', 'ln_b1')}
    del _L1_gnn_all
    return {'x': x, 'src': src, 'dst': dst, 'L0_gnn_W_self1': _L0_gnn_in['W_self1'], 'L0_gnn_W_neigh1': _L0_gnn_in['W_neigh1'], 'L0_gnn_b1': _L0_gnn_in['b1'], 'L0_gnn_W_self2': _L0_gnn_in['W_self2'], 'L0_gnn_W_neigh2': _L0_gnn_in['W_neigh2'], 'L0_gnn_b2': _L0_gnn_in['b2'], 'L1_gnn_W_pre0': _L1_gnn_in['W_pre0'], 'L1_gnn_b_pre0': _L1_gnn_in['b_pre0'], 'L1_gnn_W_post0': _L1_gnn_in['W_post0'], 'L1_gnn_b_post0': _L1_gnn_in['b_post0'], 'L1_gnn_W_lin0': _L1_gnn_in['W_lin0'], 'L1_gnn_b_lin0': _L1_gnn_in['b_lin0'], 'L1_gnn_ln_w0': _L1_gnn_in['ln_w0'], 'L1_gnn_ln_b0': _L1_gnn_in['ln_b0'], 'L1_gnn_W_pre1': _L1_gnn_in['W_pre1'], 'L1_gnn_b_pre1': _L1_gnn_in['b_pre1'], 'L1_gnn_W_post1': _L1_gnn_in['W_post1'], 'L1_gnn_b_post1': _L1_gnn_in['b_post1'], 'L1_gnn_W_lin1': _L1_gnn_in['W_lin1'], 'L1_gnn_b_lin1': _L1_gnn_in['b_lin1'], 'L1_gnn_ln_w1': _L1_gnn_in['ln_w1'], 'L1_gnn_ln_b1': _L1_gnn_in['ln_b1']}

def reference(x, src, dst, L0_gnn_W_self1, L0_gnn_W_neigh1, L0_gnn_b1, L0_gnn_W_self2, L0_gnn_W_neigh2, L0_gnn_b2, L1_gnn_W_pre0, L1_gnn_b_pre0, L1_gnn_W_post0, L1_gnn_b_post0, L1_gnn_W_lin0, L1_gnn_b_lin0, L1_gnn_ln_w0, L1_gnn_ln_b0, L1_gnn_W_pre1, L1_gnn_b_pre1, L1_gnn_W_post1, L1_gnn_b_post1, L1_gnn_W_lin1, L1_gnn_b_lin1, L1_gnn_ln_w1, L1_gnn_ln_b1):
    import jax
    import jax.numpy as jnp

    def _L0_gnn_ref(x, src, dst, W_self1, W_neigh1, b1, W_self2, W_neigh2, b2):
        import jax, jax.numpy as jnp
        import numpy as np
        N_NODES = 3125
        N_EDGES = 50000
        IN_FEATS = 128
        H_FEATS = 128

        def _sage_conv(x, src, dst, W_neigh, W_self, b):
            msg = x[src]
            summed = jax.ops.segment_sum(msg, dst, num_segments=N_NODES)
            deg = jax.ops.segment_sum(jnp.ones((src.shape[0],), x.dtype), dst, num_segments=N_NODES)
            mean = summed / jnp.maximum(deg, 1.0)[:, None]
            return x @ W_self + mean @ W_neigh + b
        h = _sage_conv(x, src, dst, W_neigh1, W_self1, b1)
        h = jax.nn.relu(h)
        h = _sage_conv(h, src, dst, W_neigh2, W_self2, b2)
        return h

    def _L1_gnn_ref(x, edge_index, W_pre0, b_pre0, W_post0, b_post0, W_lin0, b_lin0, ln_w0, ln_b0, W_pre1, b_pre1, W_post1, b_post1, W_lin1, b_lin1, ln_w1, ln_b1):
        import jax, jax.numpy as jnp
        import numpy as np
        N, E, F = (3125, 50000, 128)
        EPS_VAR = 1e-05
        EPS_LN = 1e-05

        def _layer_norm(x, w, b):
            m = jnp.mean(x, axis=-1, keepdims=True)
            v = jnp.mean((x - m) ** 2, axis=-1, keepdims=True)
            return (x - m) * jax.lax.rsqrt(v + EPS_LN) * w + b

        def _pna_conv(x, src, dst, deg, avg_log, W_pre, b_pre, W_post, b_post, W_lin, b_lin):
            Fin = x.shape[1]
            xi = x @ W_pre[:Fin]
            xj = x @ W_pre[Fin:]
            h = xi[dst] + xj[src] + b_pre
            degc = jnp.maximum(deg, 1.0)[:, None]
            mean = jax.ops.segment_sum(h, dst, N) / degc
            mean_sq = jax.ops.segment_sum(h * h, dst, N) / degc
            std = jnp.sqrt(jax.nn.relu(mean_sq - mean * mean) + EPS_VAR)
            mx = jax.ops.segment_max(h, dst, N)
            mn = jax.ops.segment_min(h, dst, N)
            has_nbr = (deg > 0)[:, None]
            mx = jnp.where(has_nbr, mx, 0.0)
            mn = jnp.where(has_nbr, mn, 0.0)
            agg = jnp.concatenate([mean, mx, mn, std], axis=-1)
            amp = jnp.log(degc + 1.0) / avg_log
            att = avg_log / jnp.log(degc + 1.0)
            out = jnp.concatenate([agg, agg * amp, agg * att], axis=-1)
            out = jnp.concatenate([x, out], axis=-1) @ W_post + b_post
            return out @ W_lin + b_lin
        src, dst = (edge_index[0], edge_index[1])
        deg = jax.ops.segment_sum(jnp.ones(src.shape, x.dtype), dst, N)
        avg_log = jnp.mean(jnp.log(deg + 1.0))
        h = _pna_conv(x, src, dst, deg, avg_log, W_pre0, b_pre0, W_post0, b_post0, W_lin0, b_lin0)
        h = jax.nn.relu(_layer_norm(h, ln_w0, ln_b0)) + x
        h2 = _pna_conv(h, src, dst, deg, avg_log, W_pre1, b_pre1, W_post1, b_post1, W_lin1, b_lin1)
        h2 = _layer_norm(h2, ln_w1, ln_b1) + h
        return h2
    edge_index = jnp.stack([src, dst])
    x = _layernorm(x + _L0_gnn_ref(x, src, dst, L0_gnn_W_self1, L0_gnn_W_neigh1, L0_gnn_b1, L0_gnn_W_self2, L0_gnn_W_neigh2, L0_gnn_b2), axis=-1)
    x = _layernorm(x + _L1_gnn_ref(x, edge_index, L1_gnn_W_pre0, L1_gnn_b_pre0, L1_gnn_W_post0, L1_gnn_b_post0, L1_gnn_W_lin0, L1_gnn_b_lin0, L1_gnn_ln_w0, L1_gnn_ln_b0, L1_gnn_W_pre1, L1_gnn_b_pre1, L1_gnn_W_post1, L1_gnn_b_post1, L1_gnn_W_lin1, L1_gnn_b_lin1, L1_gnn_ln_w1, L1_gnn_ln_b1), axis=-1)
    return x

_drawn_inputs = setup_inputs


def setup_inputs(seed=0):
    import zlib

    import numpy as np

    out = dict(_drawn_inputs(seed))
    spreads = {'L0_gnn_b1': (0.0, 0.1),
     'L0_gnn_b2': (0.0, 0.1),
     'L1_gnn_b_pre0': (0.0, 0.278),
     'L1_gnn_b_post0': (0.0, 0.436),
     'L1_gnn_b_lin0': (0.0, 0.281),
     'L1_gnn_ln_w0': (1.0, 0.2),
     'L1_gnn_ln_b0': (0.0, 0.1),
     'L1_gnn_b_pre1': (0.0, 0.275),
     'L1_gnn_b_post1': (0.0, 0.582),
     'L1_gnn_b_lin1': (0.0, 0.268),
     'L1_gnn_ln_w1': (1.0, 0.2),
     'L1_gnn_ln_b1': (0.0, 0.1)}
    factors = {}
    for name, (base, spread) in spreads.items():
        noise = np.random.default_rng([zlib.crc32(name.encode()), seed]).standard_normal(out[name].shape)
        drawn = base * np.exp(spread * noise) if base else spread * noise
        out[name] = jnp.asarray(drawn.astype(out[name].dtype))
    for name, factor in factors.items():
        out[name] = (out[name] * factor).astype(out[name].dtype)
    return out
```

```python
import concourse.bass as bass
from concourse import mybir
from contextlib import ExitStack

F32 = mybir.dt.float32
I32 = mybir.dt.int32
ALU = mybir.AluOpType
ACT = mybir.ActivationFunctionType
AX = mybir.AxisListType

P = 128
F = 128
N = 3125
E = 100000
NT = -(-N // P)
LAST = N - (NT - 1) * P
WIN = 14
STEPS = 784
NIT = STEPS // (2 * WIN)
RUN_TAIL = E - (P - 1) * STEPS
SAMPLE = 200
NS = E // SAMPLE
NG = 5
GT = NT // NG
BIG = 3.0e38
OUT_OF_RANGE = 1.0e6
EPS = 1.0e-5
assert STEPS % (2 * WIN) == 0 and P * STEPS >= E and E % SAMPLE == 0 and NG * GT == NT

SUM, EXTREME = 0, 1
PASSES = [SUM, SUM, SUM, EXTREME, SUM, EXTREME]
DENSE = ["sage0", "sage1", "pre0", "post0", "pre1", "post1"]
ITEMS = {"sage0": 2, "sage1": 2, "pre0": 1, "post0": 6, "pre1": 1, "post1": 6}
ITEM_BASE = {d: 1 + NG * sum(ITEMS[c] for c in DENSE[:i]) for i, d in enumerate(DENSE)}
EVAC = {"sage0": 1, "sage1": 1, "pre0": 2, "post0": 2, "pre1": 2, "post1": 2}
EVAC_BASE = {d: 1 + NG * sum(EVAC[c] for c in DENSE[:i]) for i, d in enumerate(DENSE)}
W_SAGE, W_PRE, W_LIN, W_POST = [0, 2], [4, 6], [8, 9], [10, 23]
NW = 36
V_B, V_BPRE, V_BPOST, V_BLIN, V_LNW, V_LNB = [0, 1], [2, 7], [3, 8], [4, 9], [5, 10], [6, 11]
NV = 12
SCAN0 = 4 * WIN


def gnn_kernel(nc, x, src, dst, w_self1, w_neigh1, b1, w_self2, w_neigh2, b2,
               w_pre0, b_pre0, w_post0, b_post0, w_lin0, b_lin0, ln_w0, ln_b0,
               w_pre1, b_pre1, w_post1, b_post1, w_lin1, b_lin1, ln_w1, ln_b1, out):
    ctx = ExitStack()
    with ctx:
        def sb(name, shape, dt=F32):
            return ctx.enter_context(nc.sbuf_tensor(name, shape, dt))

        def sem(name):
            return ctx.enter_context(nc.semaphore(name))

        tables = [nc.dram_tensor(f"table{i}", [NT * P, F], F32).ap() for i in range(3)]
        history = nc.dram_tensor("history", [P * STEPS, 2 * F], F32).ap()

        X = sb("X", [P, NT, F])
        H = sb("H", [P, NT, F])
        C = sb("C", [P, NT, F])
        MEAN = sb("MEAN", [P, NT, F])
        STD = sb("STD", [P, NT, F])
        Y = sb("Y", [P, NT, F])
        EXT = sb("EXT", [P, NT, 2 * F])
        rows = sb("rows", [P, 2, WIN, F])
        squares = sb("squares", [P, 2, WIN, F])
        hist = sb("hist", [P, 2, WIN, 2 * F])
        idx = sb("idx", [P, STEPS], I32)
        stage = sb("stage", [P, 2, WIN], I32)
        keep = sb("keep", [P, STEPS])
        neg = sb("neg", [P, STEPS])
        pos = sb("pos", [P, STEPS])
        weights = sb("weights", [P, NW, F])
        vectors = sb("vectors", [P, NV, F])
        ident = sb("ident", [P, P])
        ones = sb("ones", [P, P])
        shift = sb("shift", [P, P])
        wrap = sb("wrap", [P, P])
        runm = sb("runm", [P, 3, P])
        cin = sb("cin", [P, 2, P + 1])
        fix = sb("fix", [P, 2, 2 * F])
        lhs = sb("lhs", [P, 2, GT * P])
        small = sb("small", [P, 16, NT])
        tiny = sb("tiny", [P, 16])
        icol = sb("icol", [P, 3, NT], I32)
        dstI = H[:].rearrange("p a b -> p (a b)").bitcast(I32)[:, 0:STEPS + 2]
        dstF = C[:].rearrange("p a b -> p (a b)")[:, 0:STEPS + 2]
        restart = C[:].rearrange("p a b -> p (a b)")[:, STEPS + 8:2 * STEPS + 8]
        ends = C[:].rearrange("p a b -> p (a b)")[:, 2 * STEPS + 16:3 * STEPS + 16]
        kpos = H[:].rearrange("p a b -> p (a b)")[:, STEPS + 8:2 * STEPS + 8]
        kposI = H[:].rearrange("p a b -> p (a b)").bitcast(I32)[:, 2 * STEPS + 16:3 * STEPS + 16]
        sampI = MEAN[:].rearrange("p a b -> p (a b)").bitcast(I32)[0:1, 0:NS]
        sampF = MEAN[:].rearrange("p a b -> p (a b)")[0:1, NS:2 * NS]
        samples = MEAN[:].rearrange("p a b -> p (a b)")[:, 2 * NS:3 * NS]
        junk = Y[:].rearrange("p a b -> p (a b)")[:, 0:GT * NS].rearrange("p (a b) -> p a b", b=NS)
        chunks = EXT[:].rearrange("p a b -> p (a b)").bitcast(I32)[:, 0:NT * SAMPLE]\
            .rearrange("p (a b) -> p a b", b=SAMPLE)
        nodeI = icol[:, 0, :]
        chunkI = icol[:, 1, :]
        endI = icol[:, 2, :]
        fixI = sb("fixI", [P, 1], I32)
        (NODE, CNT, CHUNK, LE, LT, HAS, DEGC, RDEG, LOGD, AMP, ATT, M0, M1, M2, LOG1) = \
            [small[:, i, :] for i in range(15)]

        acc = ctx.enter_context(nc.psum_tensor("acc", [P, GT, 512], F32))
        turn = ctx.enter_context(nc.psum_tensor("turn", [P, 2, 512], F32))
        turnf = turn[:].rearrange("p a b -> p (a b)")

        consts = sem("consts")
        pool_chain = sem("pool_chain")
        x_in = sem("x_in")
        edges_in = sem("edges_in")
        weights_in = sem("weights_in")
        padded = sem("padded")
        dve_chain = sem("dve_chain")
        smp_ready = sem("smp_ready")
        small_mm = sem("small_mm")
        pe_go = sem("pe_go")
        chunk_ready = sem("chunk_ready")
        chunks_in = sem("chunks_in")
        fix_ready = sem("fix_ready")
        act_ask = sem("act_ask")
        act_did = sem("act_did")
        table_ready = sem("table_ready")
        table_in = sem("table_in")
        staged = sem("staged")
        window_opened = sem("window_opened")
        landed = [sem("landed0"), sem("landed1")]
        scan_ops = sem("scan_ops")
        squared = sem("squared")
        stored = [sem("stored0"), sem("stored1")]
        tail_turned = sem("tail_turned")
        carry = sem("carry")
        carry_turned = sem("carry_turned")
        first_in = sem("first_in")
        fixed = sem("fixed")
        fix_out = sem("fix_out")
        ext_in = sem("ext_in")
        ext_free = sem("ext_free")
        dense_in = sem("dense_in")
        u_ready = sem("u_ready")
        loop_chain = sem("loop_chain")
        turned = sem("turned")
        copied = sem("copied")
        product = sem("product")
        evac = sem("evac")
        out_ready = sem("out_ready")
        out_stored = sem("out_stored")

        block = ctx.enter_context(nc.Block())

        @block.sync
        def _(sp):
            sp.wait_ge(padded, 1)
            sp.dma_start(dstI[0:P - 1, 1:STEPS + 1],
                         dst[0:(P - 1) * STEPS].rearrange("(p k) -> p k", k=STEPS)).then_inc(edges_in, 16)
            sp.dma_start(dstI[P - 1:P, 1:RUN_TAIL + 1],
                         dst[(P - 1) * STEPS:E].rearrange("(a k) -> a k", a=1)).then_inc(edges_in, 16)
            runs = dst[0:(P - 1) * STEPS].rearrange("(p k) -> p k", k=STEPS)
            with nc.allow_non_contiguous_dma(reason="one value for each partition"):
                sp.dma_start(dstI[1:P, 0:1], runs[:, STEPS - 1:STEPS]).then_inc(edges_in, 16)
                sp.dma_start(dstI[0:P - 2, STEPS + 1:STEPS + 2], runs[1:P - 1, 0:1]).then_inc(edges_in, 16)
                sp.dma_start(dstI[P - 2:P - 1, STEPS + 1:STEPS + 2],
                             dst[(P - 1) * STEPS:(P - 1) * STEPS + 1].rearrange("(a k) -> a k", a=1))\
                    .then_inc(edges_in, 16)
                sp.dma_start(sampI, dst.rearrange("(a s k) -> a s k", a=1, k=SAMPLE)[:, :, 0])\
                    .then_inc(edges_in, 16)
            sp.dma_start(idx[0:P - 1, :],
                         src[0:(P - 1) * STEPS].rearrange("(p k) -> p k", k=STEPS)).then_inc(edges_in, 16)
            sp.dma_start(idx[P - 1:P, 0:RUN_TAIL],
                         src[(P - 1) * STEPS:E].rearrange("(a k) -> a k", a=1)).then_inc(edges_in, 16)
            sp.dma_start(X[:, 0:NT - 1, :], x[0:(NT - 1) * P, :].rearrange("(b p) f -> p b f", p=P))\
                .then_inc(x_in, 16)
            sp.dma_start(X[0:LAST, NT - 1, :], x[(NT - 1) * P:N, :]).then_inc(x_in, 16)
            for w in range(2):
                sp.dma_start(history[0:P * WIN, :].rearrange("(p s) f -> p (s f)", s=WIN),
                             hist[:, w].rearrange("p s f -> p (s f)")).then_inc(stored[w], 16)
                sp.wait_ge(stored[w], 16)
            hist_v = history.rearrange("(p k) f -> p (k f)", k=STEPS)
            tabled = 0
            for g, kind in enumerate(PASSES):
                if g in (1, 2, 4):
                    sp.wait_ge(table_ready, tabled + 1)
                    source = (H, Y, Y)[tabled]
                    sp.dma_start(tables[tabled].rearrange("(b p) f -> p b f", p=P), source[:])\
                        .then_inc(table_in, 16)
                    tabled += 1
                if g > 0:
                    sp.wait_ge(ext_in, 16 * NT * g)
                with sp.Fori(0, NIT) as it:
                    for w in range(2):
                        sp.wait_ge(scan_ops, it * (4 * WIN) + (SCAN0 + 2 * WIN * (2 * NIT * g + w + 1)))
                        sp.dma_start(hist_v[:, bass.ds((it * 2 + w) * (WIN * 2 * F), WIN * 2 * F)],
                                     hist[:, w].rearrange("p s f -> p (s f)")).then_inc(stored[w], 16)
            sp.wait_ge(out_ready, 1)
            sp.dma_start(out[0:(NT - 1) * P, :].rearrange("(b p) f -> p b f", p=P), Y[:, 0:NT - 1, :])\
                .then_inc(out_stored, 16)
            sp.dma_start(out[(NT - 1) * P:N, :], Y[0:LAST, NT - 1, :]).then_inc(out_stored, 16)
            sp.wait_ge(out_stored, 32)
            sp.wait_ge(fix_out, 16 * len(PASSES))

        @block.scalar
        def _(act):
            for w, at in ((w_self1, 0), (w_neigh1, 1), (w_self2, 2), (w_neigh2, 3), (w_lin0, 8), (w_lin1, 9)):
                act.dma_start(weights[:, at, :], w).then_inc(weights_in, 16)
            for l, w in enumerate((w_pre0, w_pre1)):
                act.dma_start(weights[:, W_PRE[l]:W_PRE[l] + 2, :], w.rearrange("(a p) f -> p a f", p=P))\
                    .then_inc(weights_in, 16)
            for l, w in enumerate((w_post0, w_post1)):
                at = W_POST[l]
                act.dma_start(weights[:, at, :], w[0:F, :]).then_inc(weights_in, 16)
                for j in range(3):
                    act.dma_start(weights[:, at + 1 + j:at + 11 + j:3, :],
                                  w[(1 + 4 * j) * F:(5 + 4 * j) * F, :].rearrange("(a p) f -> p a f", p=P))\
                        .then_inc(weights_in, 16)
            for i, v in enumerate((b1, b2, b_pre0, b_post0, b_lin0, ln_w0, ln_b0, b_pre1, b_post1, b_lin1,
                                   ln_w1, ln_b1)):
                act.dma_start(vectors[:, i, :], v.partition_broadcast(P)).then_inc(weights_in, 16)
            act.sem_inc(copied, 1)
            asked = [0]

            def function(o, i, func):
                asked[0] += 1
                act.wait_ge(act_ask, asked[0])
                nc.scalar.activation(o, i, func).then_inc(act_did, 1)

            def dense(d):
                n = ITEMS[d]
                with act.Fori(0, NG) as g:
                    for q in range(n):
                        item = g * n + (ITEM_BASE[d] + q)
                        act.wait_ge(turned, g * n + (ITEM_BASE[d] + q))
                        act.wait_ge(product, item if q == 0 else g * n + (ITEM_BASE[d] + q - 1))
                        nc.scalar.copy(lhs[:, q % 2, :], turnf[:, 0:GT * P]).then_inc(copied, 1)

            def squares_of(g, sums):
                with act.Fori(0, NIT) as it:
                    for w in range(2):
                        act.wait_ge(landed[w], it * (16 * WIN) + 16 * WIN * (NIT * g + 1))
                        act.wait_ge(scan_ops, it * (4 * WIN) + (SCAN0 + 2 * WIN * (2 * NIT * g + w - 1)))
                        nc.scalar.activation(squares[:, w].rearrange("p s f -> p (s f)"),
                                             rows[:, w].rearrange("p s f -> p (s f)"), ACT.Square)\
                            .then_inc(squared, 1)

            sqrts = lambda: function(M2, M1, ACT.Sqrt)
            function(LOGD, DEGC, ACT.Ln)
            function(LOG1, M0, ACT.Ln)
            squares_of(0, 0)
            dense("sage0")
            squares_of(1, 1)
            dense("sage1")
            sqrts()
            for l, g in ((0, 2), (1, 4)):
                dense(f"pre{l}")
                squares_of(g, g - l)
                function(STD[:], STD[:], ACT.Sqrt)
                dense(f"post{l}")
                sqrts()
            sqrts()

        @block.gpsimd
        def _(pool):
            nc.gpsimd.memset(ident[:], 0.0).then_inc(pool_chain, 1)
            nc.gpsimd.memset(shift[:], 0.0).then_inc(pool_chain, 1)
            nc.gpsimd.memset(wrap[:], 0.0).then_inc(pool_chain, 1)
            nc.gpsimd.memset(ones[:], 1.0).then_inc(consts, 1)
            nc.gpsimd.iota(nodeI, pattern=[[P, NT]], base=0, channel_multiplier=1).then_inc(consts, 1)
            nc.gpsimd.iota(kposI, pattern=[[1, STEPS]], base=0, channel_multiplier=0).then_inc(consts, 1)
            pool.wait_ge(pool_chain, 3)
            nc.gpsimd.affine_select(out=ident[:], in_=ident[:], compare_op=ALU.not_equal, fill=1.0,
                                    base=0, pattern=[[-1, P]], channel_multiplier=1).then_inc(consts, 1)
            nc.gpsimd.affine_select(out=shift[:], in_=shift[:], compare_op=ALU.not_equal, fill=1.0,
                                    base=1, pattern=[[-1, P]], channel_multiplier=1).then_inc(consts, 1)
            nc.gpsimd.affine_select(out=wrap[:], in_=wrap[:], compare_op=ALU.not_equal, fill=1.0,
                                    base=-(P - 1), pattern=[[P, P]], channel_multiplier=1)\
                .then_inc(consts, 1)
            pool.wait_ge(chunk_ready, 1)
            for b in range(NT):
                nc.gpsimd.indirect_dma_start(
                    out=chunks[:, b, :], out_offset=None, in_=dst.rearrange("(s k) -> s k", k=SAMPLE),
                    in_offset=bass.IndirectOffsetOnAxis(ap=chunkI[:, b:b + 1], axis=0)).then_inc(chunks_in, 16)
            pool.wait_ge(edges_in, 16 * 8)
            pool.wait_ge(fix_ready, 1)
            for g, kind in enumerate(PASSES):
                table = (x, tables[0], tables[1], tables[1], tables[2], tables[2])[g]
                if g > 0:
                    pool.wait_ge(table_in, 16 * (1, 1, 2, 2, 3, 3)[g])
                with pool.Fori(0, NIT) as it:
                    for w in range(2):
                        pool.wait_ge(scan_ops, it * (4 * WIN) + (SCAN0 + 2 * WIN * (2 * NIT * g + w - 1)))
                        nc.gpsimd.tensor_copy(stage[:, w, :], idx[:, bass.ds((it * 2 + w) * WIN, WIN)])\
                            .then_inc(staged, 1)
                        pool.wait_ge(staged, it * 2 + (2 * NIT * g + w + 1))
                        pool.sem_inc(window_opened, 1)
                        for s in range(WIN):
                            nc.gpsimd.indirect_dma_start(
                                out=rows[:, w, s, :], out_offset=None, in_=table,
                                in_offset=bass.IndirectOffsetOnAxis(ap=stage[:, w, s:s + 1], axis=0))\
                                .then_inc(landed[w], 16)
                for w in range(2):
                    pool.wait_ge(stored[w], 16 * (1 + NIT * (g + 1)))
                nc.gpsimd.indirect_dma_start(
                    out=fix[:, 0, :], out_offset=None, in_=history,
                    in_offset=bass.IndirectOffsetOnAxis(ap=fixI[:, 0:1], axis=0),
                    bounds_check=P * STEPS - 1, oob_is_err=False).then_inc(first_in, 16)
                pool.wait_ge(fixed, g + 1)
                nc.gpsimd.indirect_dma_start(
                    out=history, out_offset=bass.IndirectOffsetOnAxis(ap=fixI[:, 0:1], axis=0),
                    in_=fix[:, 1, :], in_offset=None,
                    bounds_check=P * STEPS - 1, oob_is_err=False).then_inc(fix_out, 16)
                pool.wait_ge(fix_out, 16 * (g + 1))
                pool.wait_ge(ext_free, g + 1)
                for b in range(NT):
                    nc.gpsimd.indirect_dma_start(
                        out=EXT[:, b, :], out_offset=None, in_=history,
                        in_offset=bass.IndirectOffsetOnAxis(ap=endI[:, b:b + 1], axis=0))\
                        .then_inc(ext_in, 16)

        @block.tensor
        def _(pe):
            pe.sem_inc(product, 1)
            pe.wait_ge(consts, 6)
            pe.wait_ge(pe_go, 1)
            nc.tensor.matmul(acc[:, 0, 0:NS], ones[0:1, :], sampF, start=True, stop=True).then_inc(small_mm, 1)
            pe.wait_ge(pe_go, 2)
            nc.tensor.matmul(acc[:, 1, 0:NT], shift[:], LE, start=True, stop=False)
            nc.tensor.matmul(acc[:, 1, 1:NT], wrap[:], LE[:, 0:NT - 1], start=False, stop=True)\
                .then_inc(small_mm, 1)
            pe.wait_ge(pe_go, 3)
            nc.tensor.matmul(acc[:, 2, 0:1], ones[:], tiny[:, 0:1], start=True, stop=True)
            nc.tensor.matmul(acc[:, 3, 0:P], tiny[:, 4:5].to_broadcast([P, P]), ident[:],
                             start=True, stop=True).then_inc(small_mm, 1)
            pe.wait_ge(weights_in, 16 * 28)

            def carries(g):
                pe.wait_ge(scan_ops, SCAN0 + 4 * WIN * NIT * (g + 1))
                pe.wait_ge(copied, ITEM_BASE[DENSE[(0, 1, 3, 3, 5, 5)[g]]])
                for h in range(2):
                    t = nc.tensor.transpose(turn[:, h, 0:P], hist[:, 1, WIN - 1, h * F:(h + 1) * F], ident[:])
                t.then_inc(tail_turned, 1)
                pe.wait_ge(carry, g + 1)
                for h in range(2):
                    t = nc.tensor.transpose(turn[:, h, P:2 * P], cin[:, h, 0:P], ident[:])
                t.then_inc(carry_turned, 1)

            def dense(k, d, sources, rhs, at):
                n = ITEMS[d]
                pe.wait_ge(dense_in, k + 1)
                for g in range(NG):
                    for q in range(n):
                        pe.wait_ge(copied, g * n + (ITEM_BASE[d] + q))
                        if d.startswith("post") and q == n - 1:
                            pe.wait_ge(u_ready, g + (1 + NG * (d == "post1")))
                        for t in range(GT):
                            m = nc.tensor.transpose(turnf[:, t * P:(t + 1) * P],
                                                    sources[q][:, (g * GT + t) * F:(g * GT + t + 1) * F], ident[:])
                        m.then_inc(turned, 1)
                        pe.wait_ge(copied, g * n + (ITEM_BASE[d] + q + 1))
                        if q == 0:
                            pe.wait_ge(evac, g * EVAC[d] + EVAC_BASE[d])
                        c0, c1, first, final = at[q]
                        for t in range(GT):
                            m = nc.tensor.matmul(acc[:, t, c0:c1], lhs[:, q % 2, t * P:(t + 1) * P],
                                                 weights[:, rhs[q]:rhs[q] + (c1 - c0) // F, :]
                                                 .rearrange("p a f -> p (a f)"), start=first, stop=final)
                        m.then_inc(product, 1)

            flat = lambda t: t[:].rearrange("p a f -> p (a f)")
            carries(0)
            dense(0, "sage0", [flat(X), flat(MEAN)], [W_SAGE[0], W_SAGE[0] + 1],
                  [(0, F, True, False), (0, F, False, True)])
            carries(1)
            dense(1, "sage1", [flat(H), flat(MEAN)], [W_SAGE[1], W_SAGE[1] + 1],
                  [(0, F, True, False), (0, F, False, True)])
            for l, inp in ((0, X), (1, H)):
                dense(2 + 2 * l, f"pre{l}", [flat(inp)], [W_PRE[l]], [(0, 2 * F, True, True)])
                carries(2 + 2 * l)
                carries(3 + 2 * l)
                w = W_POST[l]
                dense(3 + 2 * l, f"post{l}", [flat(MEAN), flat(inp), flat(Y), flat(C), flat(STD), flat(STD)],
                      [w + 1, w, w + 4, w + 7, w + 10, W_LIN[l]],
                      [(0, 3 * F, True, False), (0, F, False, False), (0, 3 * F, False, False),
                       (0, 3 * F, False, False), (0, 3 * F, False, True), (3 * F, 4 * F, True, True)])

        @block.vector
        def _(dve):
            v = nc.vector
            chain = [0]

            def link(ins):
                chain[0] += 1
                ins.then_inc(dve_chain, 1)
                dve.wait_ge(dve_chain, chain[0])

            asks = [0]

            def ask():
                asks[0] += 1
                dve.sem_inc(act_ask, 1)
                dve.wait_ge(act_did, asks[0])

            def over_f(t):
                return t.unsqueeze(2).to_broadcast([P, NT, F])

            def over_n(i, n=NT):
                return vectors[:, i, :].unsqueeze(1).to_broadcast([P, n, F])

            link(v.memset(dstI, -1))
            link(v.memset(idx[:], 0))
            link(v.memset(X[:, NT - 1, :], 0.0))
            link(v.memset(hist[:], 0.0))
            link(v.memset(fix[:, 0, :], 0.0))
            link(v.memset(cin[:, :, 0:1], 0.0))
            dve.sem_inc(padded, 1)
            dve.sem_inc(scan_ops, SCAN0)
            dve.sem_inc(evac, 1)
            dve.wait_ge(edges_in, 16 * 8)
            dve.wait_ge(consts, 6)
            link(v.tensor_copy(sampF, sampI))
            dve.sem_inc(pe_go, 1)
            link(v.tensor_copy(NODE, nodeI))
            dve.wait_ge(small_mm, 1)
            link(v.tensor_copy(samples, acc[:, 0, 0:NS]))
            for g in range(NG):
                link(v.tensor_tensor(junk, samples.unsqueeze(1).to_broadcast([P, GT, NS]),
                                     NODE[:, g * GT:(g + 1) * GT].unsqueeze(2).to_broadcast([P, GT, NS]),
                                     ALU.is_le))
                link(v.tensor_reduce(CNT[:, g * GT:(g + 1) * GT], junk, AX.X, ALU.add))
            link(v.tensor_scalar(CHUNK, CNT, -1.0, 0.0, ALU.add, ALU.max))
            link(v.tensor_copy(chunkI, CHUNK))
            dve.sem_inc(chunk_ready, 1)
            link(v.tensor_copy(dstF, dstI))
            link(v.tensor_copy(kpos, kposI))
            link(v.tensor_tensor(restart, dstF[:, 1:STEPS + 1], dstF[:, 0:STEPS], ALU.not_equal))
            link(v.tensor_tensor(ends, dstF[:, 1:STEPS + 1], dstF[:, 2:STEPS + 2], ALU.not_equal))
            fresh, inner, whole, kfirst, base = (tiny[:, i:i + 1] for i in (1, 2, 4, 5, 6))
            link(v.tensor_copy(fresh, restart[:, 0:1]))
            link(v.tensor_reduce(inner, restart[:, 1:STEPS], AX.X, ALU.add))
            link(v.memset(restart[:, 0:1], 1.0))
            link(v.tensor_scalar(keep[:], restart, -1.0, 1.0, ALU.mult, ALU.add))
            link(v.tensor_scalar(neg[:], restart, -BIG, None, ALU.mult))
            link(v.tensor_scalar(pos[:], restart, BIG, None, ALU.mult))
            link(v.tensor_scalar(inner, inner, 0.0, None, ALU.is_equal))
            link(v.tensor_scalar(tiny[:, 3:4], fresh, -1.0, 1.0, ALU.mult, ALU.add))
            link(v.tensor_tensor(whole, inner, tiny[:, 3:4], ALU.mult))
            link(v.tensor_scalar(ends, ends, -OUT_OF_RANGE, OUT_OF_RANGE, ALU.mult, ALU.add))
            link(v.tensor_tensor(kpos, kpos, ends, ALU.add))
            link(v.tensor_reduce(kfirst, kpos, AX.X, ALU.min))
            link(v.tensor_scalar(base, NODE[:, 0:1], float(STEPS), None, ALU.mult))
            link(v.tensor_tensor(kfirst, kfirst, base, ALU.add))
            link(v.tensor_scalar(base, fresh, OUT_OF_RANGE, None, ALU.mult))
            link(v.tensor_tensor(kfirst, kfirst, base, ALU.add))
            link(v.tensor_copy(fixI[:], kfirst))
            dve.wait_ge(chunks_in, 16 * NT)
            jc = Y[:].rearrange("p a b -> p (a b)")[:, 0:GT * SAMPLE].rearrange("p (a b) -> p a b", b=SAMPLE)
            for g in range(NG):
                link(v.tensor_tensor(jc, chunks[:, g * GT:(g + 1) * GT, :],
                                     NODE[:, g * GT:(g + 1) * GT].unsqueeze(2).to_broadcast([P, GT, SAMPLE]),
                                     ALU.is_le))
                link(v.tensor_reduce(CNT[:, g * GT:(g + 1) * GT], jc, AX.X, ALU.add))
            link(v.scalar_tensor_tensor(LE, CHUNK, float(SAMPLE), CNT, ALU.mult, ALU.add))
            link(v.tensor_scalar(M0, LE, -1.0, 0.0, ALU.add, ALU.max))
            link(v.tensor_copy(endI, M0))
            dve.sem_inc(fix_ready, 1)
            dve.sem_inc(pe_go, 1)
            dve.wait_ge(small_mm, 2)
            link(v.tensor_copy(LT, acc[:, 1, 0:NT]))
            link(v.tensor_tensor(M0, LE, LT, ALU.subtract))
            link(v.tensor_scalar(HAS, M0, 0.0, None, ALU.is_gt))
            link(v.tensor_scalar(DEGC, M0, 1.0, None, ALU.max))
            link(v.reciprocal(RDEG, DEGC))
            link(v.tensor_tensor(RDEG, RDEG, HAS, ALU.mult))
            link(v.tensor_scalar(DEGC, DEGC, 1.0, None, ALU.add))
            ask()
            link(v.tensor_scalar(M0, M0, 1.0, None, ALU.add))
            ask()
            link(v.tensor_reduce(tiny[:, 0:1], LOG1, AX.X, ALU.add))
            dve.sem_inc(pe_go, 1)
            dve.wait_ge(small_mm, 3)
            avg, ravg = tiny[:, 7:8], tiny[:, 8:9]
            link(v.tensor_scalar(avg, acc[:, 2, 0:1], 1.0 / N, None, ALU.mult))
            link(v.reciprocal(ravg, avg))
            link(v.tensor_scalar(AMP, LOGD, ravg, None, ALU.mult))
            link(v.reciprocal(ATT, LOGD))
            link(v.tensor_scalar(ATT, ATT, avg, None, ALU.mult))
            link(v.tensor_copy(runm[:, 0, :], acc[:, 3, 0:P]))
            link(v.tensor_scalar(runm[:, 1, :], runm[:, 0, :], BIG, -BIG, ALU.mult, ALU.add))
            link(v.tensor_scalar(runm[:, 2, :], runm[:, 0, :], -BIG, BIG, ALU.mult, ALU.add))
            dve.wait_ge(x_in, 32)
            dve.wait_ge(weights_in, 16 * 28)
            sums = [0]

            def scan(g):
                kind = PASSES[g]
                dve.sem_inc(ext_free, 1)
                col = keep if kind == SUM else neg
                col2 = keep if kind == SUM else pos
                o0 = ALU.mult if kind == SUM else ALU.add
                o1, o2 = (ALU.add, ALU.add) if kind == SUM else (ALU.max, ALU.min)
                with dve.Fori(0, NIT) as it:
                    for w in range(2):
                        dve.wait_ge(landed[w], it * (16 * WIN) + 16 * WIN * (NIT * g + 1))
                        if kind == SUM:
                            dve.wait_ge(squared, it * 2 + (2 * NIT * sums[0] + w + 1))
                        dve.wait_ge(stored[w], it * 16 + 16 * (1 + NIT * g))
                        for s in range(WIN):
                            dve.wait_ge(scan_ops, it * (4 * WIN)
                                        + (SCAN0 + 4 * WIN * NIT * g + 2 * WIN * w + 2 * s))
                            last = hist[:, w, s - 1, :] if s else hist[:, 1 - w, WIN - 1, :]
                            k = (it * 2 + w) * WIN + s
                            second = squares if kind == SUM else rows
                            v.scalar_tensor_tensor(hist[:, w, s, 0:F], last[:, 0:F], col[:, bass.ds(k, 1)],
                                                   rows[:, w, s, :], o0, o1).then_inc(scan_ops, 1)
                            v.scalar_tensor_tensor(hist[:, w, s, F:2 * F], last[:, F:2 * F],
                                                   col2[:, bass.ds(k, 1)], second[:, w, s, :], o0, o2)\
                                .then_inc(scan_ops, 1)
                sums[0] += kind == SUM
                dve.wait_ge(tail_turned, g + 1)
                for h, op in ((0, o1), (1, o2)):
                    m = 0 if kind == SUM else 1 + h
                    link(v.tensor_tensor_scan(cin[:, h, 1:P + 1], runm[:, m, :], turn[:, h, 0:P], 0.0,
                                              o0, op))
                dve.sem_inc(carry, 1)
                dve.wait_ge(carry_turned, g + 1)
                dve.wait_ge(first_in, 16 * (g + 1))
                for h, op in ((0, o1), (1, o2)):
                    link(v.tensor_tensor(fix[:, 1, h * F:(h + 1) * F], fix[:, 0, h * F:(h + 1) * F],
                                         turn[:, h, P:2 * P], op))
                dve.sem_inc(fixed, 1)
                dve.wait_ge(ext_in, 16 * NT * (g + 1))

            def evacuate(d, step):
                n, m = ITEMS[d], EVAC[d]
                dve.sem_inc(dense_in, 1)
                with dve.Fori(0, NG) as g:
                    dve.wait_ge(product, g * n + (ITEM_BASE[d] + n - d.startswith("post")))
                    step(g)
                dve.wait_ge(evac, EVAC_BASE[d] + NG * m)

            def tiles(t, g):
                return t[:].rearrange("p a f -> p (a f)")[:, bass.ds(g * (GT * F), GT * F)]\
                    .rearrange("p (a f) -> p a f", f=F)

            def add_bias(d, dest, bias):
                evacuate(d, lambda g: v.tensor_tensor(tiles(dest, g), acc[:, :, 0:F], over_n(bias, GT), ALU.add)
                         .then_inc(evac, 1))

            def layernorm(t):
                link(v.tensor_reduce(M0, t[:], AX.X, ALU.add))
                link(v.tensor_scalar(M0, M0, 1.0 / F, None, ALU.mult))
                link(v.tensor_tensor(t[:], t[:], over_f(M0), ALU.subtract))
                sq = EXT[:, :, 0:F]
                link(v.tensor_tensor(sq, t[:], t[:], ALU.mult))
                link(v.tensor_reduce(M1, sq, AX.X, ALU.add))
                link(v.tensor_scalar(M1, M1, 1.0 / F, EPS, ALU.mult, ALU.add))
                ask()
                link(v.reciprocal(M0, M2))
                link(v.tensor_tensor(t[:], t[:], over_f(M0), ALU.mult))

            scan(0)
            link(v.tensor_tensor(MEAN[:], EXT[:, :, 0:F], over_f(RDEG), ALU.mult))
            add_bias("sage0", H, V_B[0])
            link(v.tensor_scalar(H[:], H[:], 0.0, None, ALU.max))
            dve.sem_inc(table_ready, 1)
            scan(1)
            link(v.tensor_tensor(MEAN[:], EXT[:, :, 0:F], over_f(RDEG), ALU.mult))
            add_bias("sage1", Y, V_B[1])
            link(v.tensor_tensor(X[:], X[:], Y[:], ALU.add))
            layernorm(X)

            for l, inp in ((0, X), (1, H)):
                d = f"pre{l}"

                def split(g):
                    v.tensor_tensor(tiles(C, g), acc[:, :, 0:F], over_n(V_BPRE[l], GT), ALU.add)\
                        .then_inc(evac, 1)
                    v.tensor_copy(tiles(Y, g), acc[:, :, F:2 * F]).then_inc(evac, 1)

                evacuate(d, split)
                dve.sem_inc(table_ready, 1)
                scan(2 + 2 * l)
                link(v.tensor_tensor(MEAN[:], EXT[:, :, 0:F], over_f(RDEG), ALU.mult))
                link(v.tensor_tensor(STD[:], EXT[:, :, F:2 * F], over_f(RDEG), ALU.mult))
                link(v.tensor_tensor(EXT[:, :, 0:F], MEAN[:], MEAN[:], ALU.mult))
                link(v.tensor_tensor(STD[:], STD[:], EXT[:, :, 0:F], ALU.subtract))
                link(v.tensor_scalar(STD[:], STD[:], 0.0, EPS, ALU.max, ALU.add))
                ask()
                link(v.tensor_tensor(C[:], C[:], over_f(HAS), ALU.mult))
                link(v.tensor_tensor(MEAN[:], MEAN[:], C[:], ALU.add))
                scan(3 + 2 * l)
                for h, dest in ((0, Y), (1, C)):
                    link(v.tensor_tensor(EXT[:, :, h * F:(h + 1) * F], EXT[:, :, h * F:(h + 1) * F],
                                         over_f(HAS), ALU.mult))
                    link(v.tensor_tensor(dest[:], EXT[:, :, h * F:(h + 1) * F], C[:], ALU.add))
                d = f"post{l}"

                def finish(g):
                    u = tiles(STD, g)
                    v.tensor_tensor(u, acc[:, :, 0:F], over_n(V_BPOST[l], GT), ALU.add).then_inc(loop_chain, 1)
                    for j, scaler in ((1, AMP), (2, ATT)):
                        sc = scaler[:, bass.ds(g * GT, GT)].unsqueeze(2).to_broadcast([P, GT, F])
                        tmp = EXT[:, 0:GT, (j - 1) * F:j * F]
                        v.tensor_tensor(tmp, acc[:, :, j * F:(j + 1) * F], sc, ALU.mult).then_inc(loop_chain, 1)
                    n0 = 5 * NG * l
                    dve.wait_ge(loop_chain, g * 5 + (n0 + 3))
                    v.tensor_tensor(u, u, EXT[:, 0:GT, 0:F], ALU.add).then_inc(loop_chain, 1)
                    dve.wait_ge(loop_chain, g * 5 + (n0 + 4))
                    v.tensor_tensor(u, u, EXT[:, 0:GT, F:2 * F], ALU.add).then_inc(loop_chain, 1)
                    dve.wait_ge(loop_chain, g * 5 + (n0 + 5))
                    dve.sem_inc(u_ready, 1)
                    dve.sem_inc(evac, 1)
                    dve.wait_ge(product, g * ITEMS[d] + (ITEM_BASE[d] + ITEMS[d]))
                    v.tensor_tensor(tiles(Y, g), acc[:, :, 3 * F:4 * F], over_n(V_BLIN[l], GT), ALU.add)\
                        .then_inc(evac, 1)

                evacuate(d, finish)
                layernorm(Y)
                link(v.tensor_tensor(Y[:], Y[:], over_n(V_LNW[l]), ALU.mult))
                link(v.tensor_tensor(Y[:], Y[:], over_n(V_LNB[l]), ALU.add))
                if l == 0:
                    link(v.tensor_scalar(Y[:], Y[:], 0.0, None, ALU.max))
                    link(v.tensor_tensor(H[:], Y[:], X[:], ALU.add))
            link(v.tensor_tensor(Y[:], Y[:], H[:], ALU.add))
            link(v.tensor_tensor(Y[:], Y[:], X[:], ALU.add))
            layernorm(Y)
            dve.sem_inc(out_ready, 1)


_INS = ['x', 'src', 'dst', 'L0_gnn_W_self1', 'L0_gnn_W_neigh1', 'L0_gnn_b1', 'L0_gnn_W_self2', 'L0_gnn_W_neigh2',
        'L0_gnn_b2', 'L1_gnn_W_pre0', 'L1_gnn_b_pre0', 'L1_gnn_W_post0', 'L1_gnn_b_post0', 'L1_gnn_W_lin0',
        'L1_gnn_b_lin0', 'L1_gnn_ln_w0', 'L1_gnn_ln_b0', 'L1_gnn_W_pre1', 'L1_gnn_b_pre1', 'L1_gnn_W_post1',
        'L1_gnn_b_post1', 'L1_gnn_W_lin1', 'L1_gnn_b_lin1', 'L1_gnn_ln_w1', 'L1_gnn_ln_b1']


def kernel(**inputs):
    import numpy as np
    import concourse.bacc as bacc
    from concourse.bass_utils import run_bass_kernel_spmd

    nc = bacc.Bacc("TRN2", target_bir_lowering=False, num_devices=1)
    arrays, args = {}, []
    for name in _INS:
        a = np.ascontiguousarray(inputs[name])
        arrays[f"in_{name}"] = a
        args.append(nc.dram_tensor(f"in_{name}", a.shape, mybir.dt.from_np(a.dtype), kind="ExternalInput").ap())
    out = nc.dram_tensor("out", (N, F), F32, kind="ExternalOutput").ap()
    gnn_kernel(nc, *args, out)
    return run_bass_kernel_spmd(nc, [arrays], core_ids=[0]).results[0]["out"]
```

```python
import concourse.bass as bass
from concourse import mybir
from contextlib import ExitStack

F32 = mybir.dt.float32
I32 = mybir.dt.int32
BF16 = mybir.dt.bfloat16
F16 = mybir.dt.float16
ALU = mybir.AluOpType
ACT = mybir.ActivationFunctionType
AX = mybir.AxisListType

P = 128
F = 128
N = 3125
E = 100000
NT = -(-N // P)
LAST = N - (NT - 1) * P
WIN = 14
STEPS = 784
NIT = STEPS // (2 * WIN)
RUN_TAIL = E - (P - 1) * STEPS
SAMPLE = 200
NS = E // SAMPLE
NG = 5
GT = NT // NG
BIG = 3.0e38
OUT_OF_RANGE = 1.0e6
EPS = 1.0e-5
assert STEPS % (2 * WIN) == 0 and P * STEPS >= E and E % SAMPLE == 0 and NG * GT == NT

SLICE = 16
PER_BLOCK = P // SLICE
WT = 5
CODES = NT * SLICE
WINDOW = WT * P
MAX_COUNT = 250
REC_PAD = WINDOW
FLAG_FROM = 0.5
assert NT * PER_BLOCK * CODES < 2 ** 24

SUM, EXTREME = 0, 1
DENSE = ["sage0", "sage1", "pre0", "post0", "pre1", "post1"]
ITEMS = {"sage0": 2, "sage1": 2, "pre0": 1, "post0": 6, "pre1": 1, "post1": 6}
ITEM_BASE = {d: 1 + NG * sum(ITEMS[c] for c in DENSE[:i]) for i, d in enumerate(DENSE)}
EVAC = {"sage0": 1, "sage1": 1, "pre0": 2, "post0": 2, "pre1": 2, "post1": 2}
EVAC_BASE = {d: 1 + NG * sum(EVAC[c] for c in DENSE[:i]) for i, d in enumerate(DENSE)}
W_SAGE, W_PRE, W_LIN, W_POST = [0, 2], [4, 6], [8, 9], [10, 23]
NW = 36
V_B, V_BPRE, V_BPOST, V_BLIN, V_LNW, V_LNB = [0, 1], [2, 7], [3, 8], [4, 9], [5, 10], [6, 11]
NV = 12
SCAN0 = 4 * WIN


def gnn_kernel(nc, x, src, dst, w_self1, w_neigh1, b1, w_self2, w_neigh2, b2,
               w_pre0, b_pre0, w_post0, b_post0, w_lin0, b_lin0, ln_w0, ln_b0,
               w_pre1, b_pre1, w_post1, b_post1, w_lin1, b_lin1, ln_w1, ln_b1, out):
    ctx = ExitStack()
    with ctx:
        def sb(name, shape, dt=F32):
            return ctx.enter_context(nc.sbuf_tensor(name, shape, dt))

        def sem(name):
            return ctx.enter_context(nc.semaphore(name))

        tables = [nc.dram_tensor(f"table{i}", [NT * P, F], F32).ap() for i in range(3)]
        history = nc.dram_tensor("history", [P * STEPS, 2 * F], F32).ap()
        records = nc.dram_tensor("records", [(P * STEPS + REC_PAD) * 2], F32).ap()
        starts = nc.dram_tensor("starts", [2 * P], I32).ap()
        counts = nc.dram_tensor("counts", [NT, P, NT * P], BF16).ap()
        spill = nc.dram_tensor("spill", [P, NT * 2 * F], F32).ap()

        X = sb("X", [P, NT, F])
        H = sb("H", [P, NT, F])
        C = sb("C", [P, NT, F])
        Y = sb("Y", [P, NT, F])
        MS = sb("MS", [P, 2, NT, F])
        MEAN, STD = MS[:, 0], MS[:, 1]
        big = sb("big", [P, NT * 3 * F])
        XS = big[:].bitcast(BF16).rearrange("p (a c f) -> p a c f", c=3, f=2 * F)
        EXT = big[:, 0:NT * 2 * F].rearrange("p (a f) -> p a f", f=2 * F)
        A = sb("A", [P, 2, NT, P], BF16)
        rows = sb("rows", [P, 2, WIN, F])
        rowsf = rows[:].rearrange("p w s f -> p (w s f)")
        hist = sb("hist", [P, 2, WIN, 2 * F])
        histf = hist[:].rearrange("p w s f -> p (w s f)")
        idx = sb("idx", [P, STEPS + 2 * WIN], I32)
        stage = sb("stage", [P, 2, WIN], I32)
        neg = sb("neg", [P, STEPS])
        weights = sb("weights", [P, NW, F])
        vectors = sb("vectors", [P, NV, F])
        ident = sb("ident", [P, P])
        ones = sb("ones", [P, P])
        runm = sb("runm", [P, 3, P])
        cin = sb("cin", [P, 2, P + 1])
        fix = sb("fix", [P, 2, 2 * F])
        small = sb("small", [P, 16, NT])
        tiny = sb("tiny", [P, 32])
        icol = sb("icol", [P, 3, NT], I32)
        fixI = sb("fixI", [P, 1], I32)
        flagI = sb("flagI", [1, 1], I32)
        lhs = rowsf[:, 0:2 * GT * P].rearrange("p (a b) -> p a b", a=2)
        scratch = rowsf[:, 0:NT * F].rearrange("p (a b) -> p a b", b=F)
        squares = MS[:].rearrange("p m a f -> p (m a f)")[:, 0:2 * WIN * F]\
            .rearrange("p (w s f) -> p w s f", w=2, s=WIN)
        keep = A[:].rearrange("p s a d -> p (s a d)").bitcast(F32)[:, 0:STEPS]
        ONE = WT * 2
        hot_s = histf[:, 0:ONE * P // 2].bitcast(BF16).rearrange("p (h c t) -> p h c t", h=2, t=WT)
        o = ONE * P // 2
        hot_c = histf[:, o:o + ONE * CODES // 2].bitcast(BF16).rearrange("p (t c) -> p t c", c=CODES)
        o += ONE * CODES // 2
        win = histf[:, o:o + PER_BLOCK * WT * 2].rearrange("p (j t c) -> p j t c", j=PER_BLOCK, c=2)
        o += PER_BLOCK * WT * 2
        codes = histf[:, o:o + PER_BLOCK * WT].rearrange("p (j t) -> p j t", j=PER_BLOCK)
        o += PER_BLOCK * WT
        lows = histf[:, o:o + PER_BLOCK * WT // 2].bitcast(F16).rearrange("p (j t) -> p j t", j=PER_BLOCK)
        o += PER_BLOCK * WT // 2
        iota_s = histf[:, o:o + P * WT // 2].bitcast(F16).rearrange("p (c t) -> p c t", t=WT)
        o += P * WT // 2
        slice_base = histf[:, o:o + 2 * P]
        o += 2 * P
        iota_c = histf[:, o:o + CODES // 2].bitcast(F16)
        o += CODES // 2
        startrow = histf.bitcast(I32)[0:1, o:o + 2 * P]
        o += 2 * P
        assert o <= 2 * WIN * 2 * F
        hf, cf, yf = (t[:].rearrange("p a b -> p (a b)") for t in (H, C, Y))
        msf = MS[:].rearrange("p m a f -> p (m a f)")
        dstI = hf.bitcast(I32)[:, 0:STEPS + 2]
        ints1 = hf.bitcast(I32)[:, STEPS + 8:2 * STEPS + 8]
        kposI = hf.bitcast(I32)[:, 2 * STEPS + 16:3 * STEPS + 16]
        dstF = cf[:, 0:STEPS + 2]
        restart = cf[:, STEPS + 2:2 * STEPS + 2]
        ends = cf[:, 2 * STEPS + 2:3 * STEPS + 2]
        kpos = cf[:, 3 * STEPS + 2:4 * STEPS + 2]
        shift = rowsf[:, 0:P]
        wrap = rowsf[:, P:2 * P]
        jcodeI = rowsf.bitcast(I32)[:, 2 * P:2 * P + CODES]
        jsliceI = rowsf.bitcast(I32)[:, 2 * P + CODES:4 * P + CODES]
        limitI = rowsf.bitcast(I32)[:, 4 * P + CODES:4 * P + CODES + 4]
        sampI = msf.bitcast(I32)[0:1, 0:NS]
        sampF = msf[0:1, NS:2 * NS]
        samples = msf[:, 2 * NS:3 * NS]
        rec = msf[:, 3 * NS:3 * NS + 2 * STEPS].rearrange("p (k c) -> p k c", c=2)
        o = 3 * NS + 2 * STEPS
        wchunks = msf.bitcast(I32)[:, o:o + 4 * SAMPLE].rearrange("p (j k) -> p j k", k=SAMPLE)
        wjunk = yf[:, 0:4 * NS].rearrange("p (j k) -> p j k", k=NS)
        wjunk2 = yf[:, 0:4 * SAMPLE].rearrange("p (j k) -> p j k", k=SAMPLE)
        junk = yf[:, 0:GT * NS].rearrange("p (a b) -> p a b", b=NS)
        jc = yf[:, 0:GT * SAMPLE].rearrange("p (a b) -> p a b", b=SAMPLE)
        recpad = yf[:, GT * NS:GT * NS + 2 * WT]
        chunks = big[:].bitcast(I32)[:, 0:NT * SAMPLE].rearrange("p (a b) -> p a b", b=SAMPLE)
        nodeI, chunkI, endI = (icol[:, i, :] for i in range(3))
        wchunkI = fix[:, 1, 0:4].bitcast(I32)
        wstartI = fix[:, 1, 4:6].bitcast(I32)
        (NODE, CNT, CHUNK, LE, LT, HAS, DEGC, RDEG, LOGD, AMP, ATT, M0, M1, M2, LOG1) = \
            [small[:, i, :] for i in range(15)]

        acc = ctx.enter_context(nc.psum_tensor("acc", [P, GT, 512], F32))
        turn = ctx.enter_context(nc.psum_tensor("turn", [P, 2, 512], F32))
        turnf = turn[:].rearrange("p a b -> p (a b)")

        consts = sem("consts")
        pool_chain = sem("pool_chain")
        x_in = sem("x_in")
        dst_in = sem("dst_in")
        src_in = sem("src_in")
        weights_in = sem("weights_in")
        padded = sem("padded")
        dve_chain = sem("dve_chain")
        small_mm = sem("small_mm")
        pe_go = sem("pe_go")
        wchunk_ready = sem("wchunk_ready")
        wchunks_in = sem("wchunks_in")
        chunk_ready = sem("chunk_ready")
        chunks_in = sem("chunks_in")
        starts_ready = sem("starts_ready")
        starts_out = sem("starts_out")
        starts_in = sem("starts_in")
        rec_ready = sem("rec_ready")
        rec_out = sem("rec_out")
        fix_ready = sem("fix_ready")
        flag_ready = sem("flag_ready")
        act_ask = sem("act_ask")
        act_did = sem("act_did")
        table_ready = sem("table_ready")
        table_in = sem("table_in")
        table_done = sem("table_done")
        win_in = [sem(f"win_in{j}") for j in range(PER_BLOCK)]
        windows_read = sem("windows_read")
        onehots = sem("onehots")
        tallied = sem("tallied")
        counted = sem("counted")
        a_stored = [sem("a_stored0"), sem("a_stored1")]
        a_in = [sem("a_in0"), sem("a_in1")]
        parts_ready = sem("parts_ready")
        summed = sem("summed")
        sums_out = sem("sums_out")

        class ScanSems:
            def __init__(self, name):
                self.staged = sem(name + "staged")
                self.window_opened = sem(name + "window_opened")
                self.landed = [sem(name + "landed0"), sem(name + "landed1")]
                self.scan_ops = sem(name + "scan_ops")
                self.squared = sem(name + "squared")
                self.stored = [sem(name + "stored0"), sem(name + "stored1")]
                self.tail_turned = sem(name + "tail_turned")
                self.carry = sem(name + "carry")
                self.carry_turned = sem(name + "carry_turned")
                self.first_in = sem(name + "first_in")
                self.fixed = sem(name + "fixed")
                self.fix_out = sem(name + "fix_out")
                self.ext_in = sem(name + "ext_in")
                self.start = sem(name + "start")

        main = ScanSems("x_")
        general = ScanSems("g_")
        general_ask = sem("general_ask")
        general_did = sem("general_did")
        general_chain = [sem(f"general_chain{g}") for g in range(4)]
        zeroed = sem("zeroed")
        spill_ready = sem("spill_ready")
        spilled = sem("spilled")
        unspill_ready = sem("unspill_ready")
        dense_in = sem("dense_in")
        u_ready = sem("u_ready")
        loop_chain = sem("loop_chain")
        turned = sem("turned")
        copied = sem("copied")
        product = sem("product")
        evac = sem("evac")
        out_ready = sem("out_ready")
        out_stored = sem("out_stored")

        def flagged(eng):
            eng.wait_ge(flag_ready, 1)
            return eng.value_load(flagI[0:1, 0:1], min_val=0, max_val=1)

        block = ctx.enter_context(nc.Block())

        @block.sync
        def _(sp):
            sp.wait_ge(padded, 1)
            runs = dst[0:(P - 1) * STEPS].rearrange("(p k) -> p k", k=STEPS)
            with nc.allow_non_contiguous_dma(reason="one value for each partition"):
                sp.dma_start(sampI, dst.rearrange("(a s k) -> a s k", a=1, k=SAMPLE)[:, :, 0])\
                    .then_inc(dst_in, 16)
                sp.dma_start(dstI[0:P - 1, 1:STEPS + 1], runs).then_inc(dst_in, 16)
                sp.dma_start(dstI[P - 1:P, 1:RUN_TAIL + 1],
                             dst[(P - 1) * STEPS:E].rearrange("(a k) -> a k", a=1)).then_inc(dst_in, 16)
                sp.dma_start(dstI[1:P, 0:1], runs[:, STEPS - 1:STEPS]).then_inc(dst_in, 16)
                sp.dma_start(dstI[0:P - 2, STEPS + 1:STEPS + 2], runs[1:P - 1, 0:1]).then_inc(dst_in, 16)
                sp.dma_start(dstI[P - 2:P - 1, STEPS + 1:STEPS + 2],
                             dst[(P - 1) * STEPS:(P - 1) * STEPS + 1].rearrange("(a k) -> a k", a=1))\
                    .then_inc(dst_in, 16)
            sp.dma_start(idx[0:P - 1, 0:STEPS],
                         src[0:(P - 1) * STEPS].rearrange("(p k) -> p k", k=STEPS)).then_inc(src_in, 16)
            sp.dma_start(idx[P - 1:P, 0:RUN_TAIL],
                         src[(P - 1) * STEPS:E].rearrange("(a k) -> a k", a=1)).then_inc(src_in, 16)
            sp.dma_start(X[:, 0:NT - 1, :], x[0:(NT - 1) * P, :].rearrange("(b p) f -> p b f", p=P))\
                .then_inc(x_in, 16)
            sp.dma_start(X[0:LAST, NT - 1, :], x[(NT - 1) * P:N, :]).then_inc(x_in, 16)
            sp.wait_ge(rec_ready, 1)
            sp.dma_start(records[0:P * STEPS * 2].rearrange("(p q) -> p q", p=P),
                         rec.rearrange("p k c -> p (k c)")).then_inc(rec_out, 16)
            sp.dma_start(records[P * STEPS * 2:].rearrange("(p q) -> p q", p=P), recpad).then_inc(rec_out, 16)
            sp.wait_ge(starts_ready, 1)
            with nc.allow_non_contiguous_dma(reason="one value for each slice"):
                sp.dma_start(starts.rearrange("(t p) -> p t", p=P), wstartI).then_inc(starts_out, 16)
            sp.wait_ge(starts_out, 16)
            sp.dma_start(startrow, starts.rearrange("(a k) -> a k", a=1)).then_inc(starts_in, 16)
            for sems in (main, general):
                for w in range(2):
                    sp.dma_start(history[0:P, 0:P], ident[:]).then_inc(sems.stored[w], 16)
                    sp.wait_ge(sems.stored[w], 16)
            sp.wait_ge(rec_out, 32)
            sp.wait_ge(starts_in, 16)
            with sp.Fori(0, NT) as b:
                sp.wait_ge(windows_read, b * 2 + 2)
                for j in range(PER_BLOCK):
                    e = sp.value_load(startrow[0:1, bass.ds(b * PER_BLOCK + j, 1)], min_val=0, max_val=E)
                    sp.dma_start(win[:, j].rearrange("p t c -> p (t c)"),
                                 records[bass.ds(e * 2, WINDOW * 2)].rearrange("(p q) -> p q", p=P))\
                        .then_inc(win_in[j], 16)

            hist_v = history.rearrange("(p k) f -> p (k f)", k=STEPS)

            def store_history(z, g):
                sp.wait_ge(z.start, g + 1)
                with sp.Fori(0, NIT) as it:
                    for w in range(2):
                        sp.wait_ge(z.scan_ops, it * (4 * WIN) + (SCAN0 + 2 * WIN * (2 * NIT * g + w + 1)))
                        sp.dma_start(hist_v[:, bass.ds((it * 2 + w) * (WIN * 2 * F), WIN * 2 * F)],
                                     hist[:, w].rearrange("p s f -> p (s f)")).then_inc(z.stored[w], 16)

            def general_sums(g):
                with sp.If(flagged(sp)):
                    if g == 1:
                        sp.wait_ge(table_ready, 1)
                        sp.dma_start(tables[0].rearrange("(b p) f -> p b f", p=P), H[:]).then_inc(table_in, 16)
                    if g > 1:
                        sp.wait_ge(spill_ready, g - 1)
                        sp.dma_start(spill, EXT.rearrange("p a f -> p (a f)")).then_inc(spilled, 16)
                    store_history(general, g)
                    if g > 1:
                        sp.wait_ge(unspill_ready, g - 1)
                        sp.dma_start(EXT.rearrange("p a f -> p (a f)"), spill).then_inc(spilled, 16)

            general_sums(0)
            general_sums(1)
            for l in range(2):
                sp.wait_ge(table_ready, 2 + l)
                sp.dma_start(tables[1 + l].rearrange("(b p) f -> p b f", p=P), Y[:]).then_inc(table_done, 16)
                store_history(main, l)
                general_sums(2 + l)
            sp.wait_ge(out_ready, 1)
            sp.dma_start(out[0:(NT - 1) * P, :].rearrange("(b p) f -> p b f", p=P), Y[:, 0:NT - 1, :])\
                .then_inc(out_stored, 16)
            sp.dma_start(out[(NT - 1) * P:N, :], Y[0:LAST, NT - 1, :]).then_inc(out_stored, 16)
            sp.wait_ge(out_stored, 32)

        @block.scalar
        def _(act):
            for w, at in ((w_self1, 0), (w_neigh1, 1), (w_self2, 2), (w_neigh2, 3), (w_lin0, 8), (w_lin1, 9)):
                act.dma_start(weights[:, at, :], w).then_inc(weights_in, 16)
            for l, w in enumerate((w_pre0, w_pre1)):
                act.dma_start(weights[:, W_PRE[l]:W_PRE[l] + 2, :], w.rearrange("(a p) f -> p a f", p=P))\
                    .then_inc(weights_in, 16)
            for l, w in enumerate((w_post0, w_post1)):
                at = W_POST[l]
                act.dma_start(weights[:, at, :], w[0:F, :]).then_inc(weights_in, 16)
                for j in range(3):
                    act.dma_start(weights[:, at + 1 + j:at + 11 + j:3, :],
                                  w[(1 + 4 * j) * F:(5 + 4 * j) * F, :].rearrange("(a p) f -> p a f", p=P))\
                        .then_inc(weights_in, 16)
            for i, v in enumerate((b1, b2, b_pre0, b_post0, b_lin0, ln_w0, ln_b0, b_pre1, b_post1, b_lin1,
                                   ln_w1, ln_b1)):
                act.dma_start(vectors[:, i, :], v.partition_broadcast(P)).then_inc(weights_in, 16)
            act.sem_inc(copied, 1)
            act.sem_inc(counted, 2)
            act.sem_inc(sums_out, 2)
            act.wait_ge(zeroed, 1)
            for w in range(2):
                act.dma_start(counts[0, :, 0:P], A[:, w, 0, :]).then_inc(a_stored[w], 16)
                act.wait_ge(a_stored[w], 16)
            asked = [0]

            def function(o, i, func):
                asked[0] += 1
                act.wait_ge(act_ask, asked[0])
                nc.scalar.activation(o, i, func).then_inc(act_did, 1)

            def take_sums(k, b, bank, width):
                act.wait_ge(summed, b + (NT * k + 3))
                for m in range(width // F):
                    c = nc.scalar.copy(msf[:, bass.ds(b * F + m * NT * F, F)], acc[:, bank, m * F:(m + 1) * F])
                c.then_inc(sums_out, 1)

            def make_block(b, slot, first=False):
                act.wait_ge(summed, b + 1)
                act.wait_ge(a_stored[slot], (b - slot) * 8 + 16)
                for j in range(PER_BLOCK):
                    act.wait_ge(tallied, b * PER_BLOCK + (j + 3))
                    nc.scalar.copy(A[:, slot, :, j * SLICE:(j + 1) * SLICE],
                                   acc[:, j % 2, 0:CODES].rearrange("p (a d) -> p a d", d=SLICE))\
                        .then_inc(counted, 1)
                act.wait_ge(counted, b * PER_BLOCK + (PER_BLOCK + 2))
                act.dma_start(counts_v[:, bass.ds(b, 1), :].rearrange("p b q -> p (b q)"),
                              A[:, slot].rearrange("p a d -> p (a d)")).then_inc(a_stored[slot], 16)
                if not first:
                    take_sums(0, b - 1, 2 + 1 - slot, F)

            def load_block(b, slot):
                act.dma_start(A[:, slot].rearrange("p a d -> p (a d)"),
                              counts_v[:, bass.ds(b, 1), :].rearrange("p b q -> p (b q)")).then_inc(a_in[slot], 16)

            def sums(k, width):
                act.wait_ge(parts_ready, k + 1)
                load_block(0, 0)
                load_block(1, 1)
                with act.Fori(0, NT // 2 - 1) as i:
                    for s in range(2):
                        take_sums(k, i * 2 + s, s, width)
                        load_block(i * 2 + (s + 2), s)
                take_sums(k, NT - 3, 0, width)
                load_block(NT - 1, 0)
                take_sums(k, NT - 2, 1, width)
                take_sums(k, NT - 1, 0, width)

            def dense(d):
                n = ITEMS[d]
                with act.Fori(0, NG) as g:
                    for q in range(n):
                        act.wait_ge(turned, g * n + (ITEM_BASE[d] + q))
                        act.wait_ge(product, g * n + (ITEM_BASE[d] + max(q - 1, 0)))
                        nc.scalar.copy(lhs[:, q % 2, :], turnf[:, 0:GT * P]).then_inc(copied, 1)

            def squares_of(z, g):
                with act.Fori(0, NIT) as it:
                    for w in range(2):
                        act.wait_ge(z.landed[w], it * (16 * WIN) + 16 * WIN * (NIT * g + 1))
                        act.wait_ge(z.scan_ops, it * (4 * WIN) + (SCAN0 + 2 * WIN * (2 * NIT * g + w - 1)))
                        nc.scalar.activation(squares[:, w].rearrange("p s f -> p (s f)"),
                                             rows[:, w].rearrange("p s f -> p (s f)"), ACT.Square)\
                            .then_inc(z.squared, 1)

            general_asked = [0]

            def general_sums(g):
                with act.If(flagged(act)):
                    squares_of(general, g)
                    if g > 1:
                        general_asked[0] += 1
                        act.wait_ge(general_ask, general_asked[0])
                        nc.scalar.activation(STD, STD, ACT.Sqrt).then_inc(general_did, 1)

            counts_v = counts.rearrange("b p q -> p b q")
            function(LOGD, DEGC, ACT.Ln)
            function(LOG1, M0, ACT.Ln)
            make_block(0, 0, first=True)
            with act.Fori(0, NT // 2) as i:
                make_block(i * 2 + 1, 1)
                make_block(i * 2 + 2, 0)
            take_sums(0, NT - 1, 2, F)
            for w in range(2):
                act.wait_ge(a_stored[w], 16 * (1 + (NT + 1 - w) // 2))
            general_sums(0)
            dense("sage0")
            sums(1, F)
            general_sums(1)
            dense("sage1")
            function(M2, M1, ACT.Sqrt)
            for l in range(2):
                dense(f"pre{l}")
                sums(2 + l, 2 * F)
                function(STD, STD, ACT.Sqrt)
                general_sums(2 + l)
                dense(f"post{l}")
                function(M2, M1, ACT.Sqrt)
            function(M2, M1, ACT.Sqrt)

        @block.gpsimd
        def _(pool):
            nc.gpsimd.memset(ident[:], 0.0).then_inc(pool_chain, 1)
            nc.gpsimd.memset(shift, 0.0).then_inc(pool_chain, 1)
            nc.gpsimd.memset(wrap, 0.0).then_inc(pool_chain, 1)
            nc.gpsimd.memset(ones[:], 1.0).then_inc(consts, 1)
            nc.gpsimd.iota(limitI.rearrange("p (a t) -> p a t", a=2), pattern=[[SLICE, 2], [SLICE * P, 2]],
                           base=0, channel_multiplier=SLICE).then_inc(consts, 1)
            nc.gpsimd.iota(nodeI, pattern=[[P, NT]], base=0, channel_multiplier=1).then_inc(consts, 1)
            nc.gpsimd.iota(kposI, pattern=[[1, STEPS]], base=0, channel_multiplier=0).then_inc(consts, 1)
            nc.gpsimd.iota(jcodeI, pattern=[[1, CODES]], base=0, channel_multiplier=0).then_inc(consts, 1)
            nc.gpsimd.iota(jsliceI, pattern=[[CODES, 2 * P]], base=0, channel_multiplier=0).then_inc(consts, 1)
            pool.wait_ge(pool_chain, 3)
            nc.gpsimd.affine_select(out=ident[:], in_=ident[:], compare_op=ALU.not_equal, fill=1.0,
                                    base=0, pattern=[[-1, P]], channel_multiplier=1).then_inc(consts, 1)
            nc.gpsimd.affine_select(out=shift, in_=shift, compare_op=ALU.not_equal, fill=1.0,
                                    base=1, pattern=[[-1, P]], channel_multiplier=1).then_inc(consts, 1)
            nc.gpsimd.affine_select(out=wrap, in_=wrap, compare_op=ALU.not_equal, fill=1.0,
                                    base=-(P - 1), pattern=[[P, P]], channel_multiplier=1)\
                .then_inc(consts, 1)
            by_chunk = dst.rearrange("(s k) -> s k", k=SAMPLE)
            pool.wait_ge(wchunk_ready, 1)
            for t in range(4):
                nc.gpsimd.indirect_dma_start(
                    out=wchunks[:, t, :], out_offset=None, in_=by_chunk,
                    in_offset=bass.IndirectOffsetOnAxis(ap=wchunkI[:, t:t + 1], axis=0)).then_inc(wchunks_in, 16)
            pool.wait_ge(chunk_ready, 1)
            for b in range(NT):
                nc.gpsimd.indirect_dma_start(
                    out=chunks[:, b, :], out_offset=None, in_=by_chunk,
                    in_offset=bass.IndirectOffsetOnAxis(ap=chunkI[:, b:b + 1], axis=0)).then_inc(chunks_in, 16)

            def gather(z, g, table):
                pool.wait_ge(z.start, g + 1)
                with pool.Fori(0, NIT) as it:
                    for w in range(2):
                        pool.wait_ge(z.staged, it * 2 + (2 * (NIT + 1) * g + w + 1))
                        pool.sem_inc(z.window_opened, 1)
                        for s in range(WIN):
                            nc.gpsimd.indirect_dma_start(
                                out=rows[:, w, s, :], out_offset=None, in_=table,
                                in_offset=bass.IndirectOffsetOnAxis(ap=stage[:, w, s:s + 1], axis=0))\
                                .then_inc(z.landed[w], 16)
                for w in range(2):
                    pool.wait_ge(z.stored[w], 16 * (1 + NIT * (g + 1)))
                nc.gpsimd.indirect_dma_start(
                    out=fix[:, 0, :], out_offset=None, in_=history,
                    in_offset=bass.IndirectOffsetOnAxis(ap=fixI[:, 0:1], axis=0),
                    bounds_check=P * STEPS - 1, oob_is_err=False).then_inc(z.first_in, 16)
                pool.wait_ge(z.fixed, g + 1)
                nc.gpsimd.indirect_dma_start(
                    out=history, out_offset=bass.IndirectOffsetOnAxis(ap=fixI[:, 0:1], axis=0),
                    in_=fix[:, 1, :], in_offset=None,
                    bounds_check=P * STEPS - 1, oob_is_err=False).then_inc(z.fix_out, 16)
                pool.wait_ge(z.fix_out, 16 * (g + 1))
                for b in range(NT):
                    nc.gpsimd.indirect_dma_start(
                        out=EXT[:, b, :], out_offset=None, in_=history,
                        in_offset=bass.IndirectOffsetOnAxis(ap=endI[:, b:b + 1], axis=0))\
                        .then_inc(z.ext_in, 16)

            def general_sums(g):
                with pool.If(flagged(pool)):
                    if g == 1:
                        pool.wait_ge(table_in, 16)
                    gather(general, g, (x, tables[0], tables[1], tables[2])[g])

            general_sums(0)
            general_sums(1)
            for l in range(2):
                pool.wait_ge(table_done, 16 * (1 + l))
                gather(main, l, tables[1 + l])
                general_sums(2 + l)

        @block.tensor
        def _(pe):
            pe.sem_inc(product, 1)
            pe.sem_inc(tallied, 2)
            pe.sem_inc(summed, 2)
            pe.wait_ge(consts, 9)
            pe.wait_ge(pe_go, 1)
            nc.tensor.matmul(acc[:, 0, 0:NS], ones[0:1, :], sampF, start=True, stop=True).then_inc(small_mm, 1)
            pe.wait_ge(pe_go, 2)
            nc.tensor.matmul(acc[:, 3, 0:P], tiny[:, 4:5].to_broadcast([P, P]), ident[:],
                             start=True, stop=True).then_inc(small_mm, 1)
            pe.wait_ge(pe_go, 3)
            nc.tensor.matmul(acc[:, 1, 0:NT], shift, LE, start=True, stop=False)
            nc.tensor.matmul(acc[:, 1, 1:NT], wrap, LE[:, 0:NT - 1], start=False, stop=True)\
                .then_inc(small_mm, 1)
            pe.wait_ge(pe_go, 4)
            nc.tensor.matmul(acc[:, 2, 0:2], ones[:], tiny[:, 0:2], start=True, stop=True)\
                .then_inc(small_mm, 1)

            def add_block(k, b, bank, slot, width, a0, a1):
                if a0 == 0:
                    pe.wait_ge(sums_out, b + (NT * k + 1))
                for a in range(a0, a1):
                    for c in range(3):
                        m = nc.tensor.matmul(acc[:, bank, 0:width], A[:, slot, a, :], XS[:, a, c, 0:width],
                                             start=a == 0 and c == 0, stop=a == NT - 1 and c == 2)
                if a1 == NT:
                    m.then_inc(summed, 1)

            def make_block(b, slot, first=False):
                for j in range(PER_BLOCK):
                    pe.wait_ge(onehots, b * PER_BLOCK + (j + 2))
                    pe.wait_ge(counted, b * PER_BLOCK + (j + 1))
                    for t in range(WT):
                        h = (j % 2) * WT + t
                        m = nc.tensor.matmul(acc[:, j % 2, 0:CODES], hot_s[:, j % 2, :, t], hot_c[:, h, :],
                                             start=t == 0, stop=t == WT - 1)
                    m.then_inc(tallied, 1)
                    if not first:
                        if j == 0:
                            pe.wait_ge(counted, b * PER_BLOCK + 2)
                        add_block(0, b - 1, 3 - slot, 1 - slot, F,
                                  j * NT // PER_BLOCK, (j + 1) * NT // PER_BLOCK)

            pe.wait_ge(parts_ready, 1)
            make_block(0, 0, first=True)
            with pe.Fori(0, NT // 2) as i:
                make_block(i * 2 + 1, 1)
                make_block(i * 2 + 2, 0)
            pe.wait_ge(counted, NT * PER_BLOCK + 2)
            add_block(0, NT - 1, 2, 0, F, 0, NT)
            pe.wait_ge(weights_in, 16 * 28)

            def sums(k, width):
                pe.wait_ge(parts_ready, k + 1)

                def block(b, s):
                    pe.wait_ge(a_in[s], (b - s) * 8 + 16 * (1 + (k - 1) * ((NT + 1 - s) // 2)))
                    add_block(k, b, s, s, width, 0, NT)

                with pe.Fori(0, NT // 2) as i:
                    block(i * 2, 0)
                    block(i * 2 + 1, 1)
                block(NT - 1, 0)

            def carries(z, g):
                pe.wait_ge(z.scan_ops, SCAN0 + 4 * WIN * NIT * (g + 1))
                for h in range(2):
                    t = nc.tensor.transpose(turn[:, h, 0:P], hist[:, 1, WIN - 1, h * F:(h + 1) * F], ident[:])
                t.then_inc(z.tail_turned, 1)
                pe.wait_ge(z.carry, g + 1)
                for h in range(2):
                    t = nc.tensor.transpose(turn[:, h, P:2 * P], cin[:, h, 0:P], ident[:])
                t.then_inc(z.carry_turned, 1)

            def general_sums(g):
                with pe.If(flagged(pe)):
                    carries(general, g)

            def dense(k, d, sources, rhs, at):
                n = ITEMS[d]
                pe.wait_ge(dense_in, k + 1)
                for g in range(NG):
                    for q in range(n):
                        pe.wait_ge(copied, g * n + (ITEM_BASE[d] + q))
                        if d.startswith("post") and q == n - 1:
                            pe.wait_ge(u_ready, g + (1 + NG * (d == "post1")))
                        for t in range(GT):
                            m = nc.tensor.transpose(turnf[:, t * P:(t + 1) * P],
                                                    sources[q][:, (g * GT + t) * F:(g * GT + t + 1) * F], ident[:])
                        m.then_inc(turned, 1)
                        pe.wait_ge(copied, g * n + (ITEM_BASE[d] + q + 1))
                        if q == 0:
                            pe.wait_ge(evac, g * EVAC[d] + EVAC_BASE[d])
                        c0, c1, first, final = at[q]
                        for t in range(GT):
                            m = nc.tensor.matmul(acc[:, t, c0:c1], lhs[:, q % 2, t * P:(t + 1) * P],
                                                 weights[:, rhs[q]:rhs[q] + (c1 - c0) // F, :]
                                                 .rearrange("p a f -> p (a f)"), start=first, stop=final)
                        m.then_inc(product, 1)

            flat = lambda t: t[:].rearrange("p a f -> p (a f)")
            general_sums(0)
            dense(0, "sage0", [flat(X), flat(MEAN)], [W_SAGE[0], W_SAGE[0] + 1],
                  [(0, F, True, False), (0, F, False, True)])
            sums(1, F)
            general_sums(1)
            dense(1, "sage1", [flat(H), flat(MEAN)], [W_SAGE[1], W_SAGE[1] + 1],
                  [(0, F, True, False), (0, F, False, True)])
            for l, inp in ((0, X), (1, H)):
                dense(2 + 2 * l, f"pre{l}", [flat(inp)], [W_PRE[l]], [(0, 2 * F, True, True)])
                sums(2 + l, 2 * F)
                carries(main, l)
                general_sums(2 + l)
                w = W_POST[l]
                dense(3 + 2 * l, f"post{l}", [flat(MEAN), flat(inp), flat(Y), flat(C), flat(STD), flat(STD)],
                      [w + 1, w, w + 4, w + 7, w + 10, W_LIN[l]],
                      [(0, 3 * F, True, False), (0, F, False, False), (0, 3 * F, False, False),
                       (0, 3 * F, False, False), (0, 3 * F, False, True), (3 * F, 4 * F, True, True)])

        @block.vector
        def _(dve):
            v = nc.vector
            chain = [0]

            link_sem = [dve_chain]

            def link(ins):
                chain[0] += 1
                ins.then_inc(link_sem[0], 1)
                dve.wait_ge(link_sem[0], chain[0])

            asks = [0]

            def ask():
                asks[0] += 1
                dve.sem_inc(act_ask, 1)
                dve.wait_ge(act_did, asks[0])

            def over_f(t):
                return t.unsqueeze(2).to_broadcast([P, NT, F])

            def over_n(i, n=NT):
                return vectors[:, i, :].unsqueeze(1).to_broadcast([P, n, F])

            link(v.memset(dstI, -1))
            link(v.memset(idx[:], 0))
            link(v.memset(X[:, NT - 1, :], 0.0))
            dve.sem_inc(padded, 1)
            dve.sem_inc(main.scan_ops, SCAN0)
            dve.sem_inc(general.scan_ops, SCAN0)
            dve.sem_inc(evac, 1)
            dve.sem_inc(windows_read, 2)
            dve.sem_inc(onehots, 1)
            link(v.memset(recpad, -1.0))
            link(v.memset(A[:, :, 0, :], 0.0))
            dve.sem_inc(zeroed, 1)
            link(v.memset(fix[:, 0, :], 0.0))
            link(v.memset(cin[:, :, 0:1], 0.0))
            dve.wait_ge(consts, 9)
            limits = tiny[:, 8:12]
            wcnt, wchunk, wstart = tiny[:, 12:16], tiny[:, 16:20], tiny[:, 20:24]
            link(v.tensor_copy(limits, limitI))
            link(v.tensor_copy(NODE, nodeI))
            link(v.tensor_copy(iota_c, jcodeI))
            link(v.tensor_copy(iota_s, jcodeI[:, 0:P].unsqueeze(2).to_broadcast([P, P, WT])))
            link(v.tensor_copy(slice_base, jsliceI))
            dve.wait_ge(dst_in, 16 * 6)
            link(v.tensor_copy(sampF, sampI))
            dve.sem_inc(pe_go, 1)
            dve.wait_ge(small_mm, 1)
            link(v.tensor_copy(samples, acc[:, 0, 0:NS]))
            link(v.tensor_tensor(wjunk, samples.unsqueeze(1).to_broadcast([P, 4, NS]),
                                 limits.unsqueeze(2).to_broadcast([P, 4, NS]), ALU.is_lt))
            link(v.tensor_reduce(wcnt, wjunk, AX.X, ALU.add))
            link(v.tensor_scalar(wchunk, wcnt, -1.0, 0.0, ALU.add, ALU.max))
            link(v.tensor_copy(wchunkI, wchunk))
            dve.sem_inc(wchunk_ready, 1)
            for g in range(NG):
                link(v.tensor_tensor(junk, samples.unsqueeze(1).to_broadcast([P, GT, NS]),
                                     NODE[:, g * GT:(g + 1) * GT].unsqueeze(2).to_broadcast([P, GT, NS]),
                                     ALU.is_le))
                link(v.tensor_reduce(CNT[:, g * GT:(g + 1) * GT], junk, AX.X, ALU.add))
            link(v.tensor_scalar(CHUNK, CNT, -1.0, 0.0, ALU.add, ALU.max))
            link(v.tensor_copy(chunkI, CHUNK))
            dve.sem_inc(chunk_ready, 1)
            dve.wait_ge(wchunks_in, 16 * 4)
            link(v.tensor_tensor(wjunk2, wchunks, limits.unsqueeze(2).to_broadcast([P, 4, SAMPLE]), ALU.is_lt))
            link(v.tensor_reduce(wcnt, wjunk2, AX.X, ALU.add))
            link(v.scalar_tensor_tensor(wstart, wchunk, float(SAMPLE), wcnt, ALU.mult, ALU.add))
            link(v.tensor_copy(wstartI, wstart[:, 0:2]))
            dve.sem_inc(starts_ready, 1)
            link(v.tensor_tensor(wcnt[:, 0:2], wstart[:, 2:4], wstart[:, 0:2], ALU.subtract))
            link(v.tensor_tensor(wcnt[:, 0:1], wcnt[:, 0:1], wcnt[:, 1:2], ALU.max))
            link(v.tensor_scalar(wcnt[:, 0:1], wcnt[:, 0:1], float(WINDOW), None, ALU.is_gt))
            dve.wait_ge(src_in, 32)
            own = dstI[:, 1:STEPS + 1]
            link(v.tensor_scalar(ints1, own, SLICE - 1, None, ALU.bitwise_and))
            link(v.tensor_copy(rec[:, :, 0], ints1))
            link(v.tensor_scalar(ints1, own, SLICE.bit_length() - 1, None, ALU.arith_shift_right))
            link(v.scalar_tensor_tensor(rec[:, :, 0], ints1, float(CODES), rec[:, :, 0], ALU.mult, ALU.add))
            link(v.tensor_scalar(ints1, idx[:, 0:STEPS], P.bit_length() - 1, None, ALU.arith_shift_right))
            link(v.scalar_tensor_tensor(rec[:, :, 0], ints1, float(SLICE), rec[:, :, 0], ALU.mult, ALU.add))
            link(v.tensor_scalar(ints1, idx[:, 0:STEPS], P - 1, None, ALU.bitwise_and))
            link(v.tensor_copy(rec[:, :, 1], ints1))
            dve.sem_inc(rec_ready, 1)
            link(v.tensor_copy(dstF, dstI))
            link(v.tensor_copy(kpos, kposI))
            link(v.tensor_tensor(restart, dstF[:, 1:STEPS + 1], dstF[:, 0:STEPS], ALU.not_equal))
            link(v.tensor_tensor(ends, dstF[:, 1:STEPS + 1], dstF[:, 2:STEPS + 2], ALU.not_equal))
            fresh, inner, whole, kfirst, base = (tiny[:, i:i + 1] for i in (24, 25, 4, 26, 27))
            link(v.tensor_copy(fresh, restart[:, 0:1]))
            link(v.tensor_reduce(inner, restart[:, 1:STEPS], AX.X, ALU.add))
            link(v.memset(restart[:, 0:1], 1.0))
            link(v.tensor_scalar(neg[:], restart, -BIG, None, ALU.mult))
            link(v.tensor_scalar(inner, inner, 0.0, None, ALU.is_equal))
            link(v.tensor_scalar(tiny[:, 28:29], fresh, -1.0, 1.0, ALU.mult, ALU.add))
            link(v.tensor_tensor(whole, inner, tiny[:, 28:29], ALU.mult))
            dve.sem_inc(pe_go, 1)
            link(v.tensor_scalar(ends, ends, -OUT_OF_RANGE, OUT_OF_RANGE, ALU.mult, ALU.add))
            link(v.tensor_tensor(kpos, kpos, ends, ALU.add))
            link(v.tensor_reduce(kfirst, kpos, AX.X, ALU.min))
            link(v.tensor_scalar(base, NODE[:, 0:1], float(STEPS), None, ALU.mult))
            link(v.tensor_tensor(kfirst, kfirst, base, ALU.add))
            link(v.tensor_scalar(base, fresh, OUT_OF_RANGE, None, ALU.mult))
            link(v.tensor_tensor(kfirst, kfirst, base, ALU.add))
            link(v.tensor_copy(fixI[:], kfirst))
            dve.wait_ge(small_mm, 2)
            link(v.tensor_copy(runm[:, 0, :], acc[:, 3, 0:P]))
            link(v.tensor_scalar(runm[:, 1, :], runm[:, 0, :], BIG, -BIG, ALU.mult, ALU.add))
            link(v.tensor_scalar(runm[:, 2, :], runm[:, 0, :], -BIG, BIG, ALU.mult, ALU.add))
            dve.wait_ge(chunks_in, 16 * NT)
            for g in range(NG):
                link(v.tensor_tensor(jc, chunks[:, g * GT:(g + 1) * GT, :],
                                     NODE[:, g * GT:(g + 1) * GT].unsqueeze(2).to_broadcast([P, GT, SAMPLE]),
                                     ALU.is_le))
                link(v.tensor_reduce(CNT[:, g * GT:(g + 1) * GT], jc, AX.X, ALU.add))
            link(v.scalar_tensor_tensor(LE, CHUNK, float(SAMPLE), CNT, ALU.mult, ALU.add))
            link(v.tensor_scalar(M0, LE, -1.0, 0.0, ALU.add, ALU.max))
            link(v.tensor_copy(endI, M0))
            dve.sem_inc(pe_go, 1)
            dve.wait_ge(x_in, 32)
            dve.wait_ge(rec_out, 32)

            def parts(t, at, rest):
                link(v.tensor_copy(XS[:, :, 0, at:at + F], t))
                link(v.tensor_tensor(rest, t, XS[:, :, 0, at:at + F], ALU.subtract))
                link(v.tensor_copy(XS[:, :, 1, at:at + F], rest))
                link(v.tensor_tensor(XS[:, :, 2, at:at + F], rest, XS[:, :, 1, at:at + F], ALU.subtract))

            parts(X[:], 0, Y[:])
            dve.wait_ge(small_mm, 3)
            link(v.tensor_copy(LT, acc[:, 1, 0:NT]))
            link(v.tensor_tensor(M0, LE, LT, ALU.subtract))
            link(v.tensor_reduce(tiny[:, 1:2], M0, AX.X, ALU.max))
            link(v.tensor_scalar(tiny[:, 1:2], tiny[:, 1:2], float(MAX_COUNT), None, ALU.is_gt))
            link(v.tensor_tensor(tiny[:, 1:2], tiny[:, 1:2], wcnt[:, 0:1], ALU.add))
            link(v.tensor_scalar(HAS, M0, 0.0, None, ALU.is_gt))
            link(v.tensor_scalar(DEGC, M0, 1.0, None, ALU.max))
            link(v.reciprocal(RDEG, DEGC))
            link(v.tensor_tensor(RDEG, RDEG, HAS, ALU.mult))
            link(v.tensor_scalar(DEGC, DEGC, 1.0, None, ALU.add))
            ask()
            link(v.tensor_scalar(M0, M0, 1.0, None, ALU.add))
            ask()
            link(v.tensor_reduce(tiny[:, 0:1], LOG1, AX.X, ALU.add))
            dve.sem_inc(pe_go, 1)
            dve.wait_ge(small_mm, 4)
            avg, ravg = tiny[:, 6:7], tiny[:, 7:8]
            link(v.tensor_scalar(avg, acc[:, 2, 0:1], 1.0 / N, None, ALU.mult))
            link(v.tensor_scalar(flagI[:], acc[0:1, 2, 1:2], FLAG_FROM, None, ALU.is_ge))
            dve.sem_inc(flag_ready, 1)
            dve.sem_inc(parts_ready, 1)

            with dve.Fori(0, NT) as b:
                for j in range(PER_BLOCK):
                    dve.wait_ge(win_in[j], b * 16 + 16)
                dve.wait_ge(onehots, b * PER_BLOCK + 1)
                v.tensor_tensor(codes, win[:, :, :, 0], slice_base[:, bass.ds(b * PER_BLOCK, PER_BLOCK)]
                                .unsqueeze(2).to_broadcast([P, PER_BLOCK, WT]), ALU.subtract)\
                    .then_inc(windows_read, 1)
                v.tensor_copy(lows, win[:, :, :, 1]).then_inc(windows_read, 1)
                dve.wait_ge(windows_read, b * 2 + 4)
                for j in range(PER_BLOCK):
                    dve.wait_ge(tallied, b * PER_BLOCK + (j + 1))
                    v.tensor_tensor(hot_s[:, j % 2], iota_s,
                                    lows[:, j, :].unsqueeze(1).to_broadcast([P, P, WT]), ALU.is_equal)
                    for t in range(WT):
                        m = v.tensor_scalar(hot_c[:, (j % 2) * WT + t, :], iota_c, codes[:, j, t:t + 1], None,
                                            ALU.is_equal)
                    m.then_inc(onehots, 1)
            link(v.reciprocal(ravg, avg))
            link(v.tensor_scalar(AMP, LOGD, ravg, None, ALU.mult))
            link(v.reciprocal(ATT, LOGD))
            link(v.tensor_scalar(ATT, ATT, avg, None, ALU.mult))
            dve.wait_ge(weights_in, 16 * 28)
            dve.wait_ge(sums_out, NT + 2)

            def scan(z, g, kind):
                link(v.memset(hist[:, 1, WIN - 1, :], 0.0))
                for w in range(2):
                    link(v.tensor_copy(stage[:, w, :], idx[:, w * WIN:(w + 1) * WIN]))
                dve.sem_inc(z.staged, 2)
                dve.sem_inc(z.start, 1)
                col = keep if kind == SUM else neg
                o0, o0b = (ALU.mult, ALU.mult) if kind == SUM else (ALU.add, ALU.subtract)
                o1, o2 = (ALU.add, ALU.add) if kind == SUM else (ALU.max, ALU.min)
                with dve.Fori(0, NIT) as it:
                    for w in range(2):
                        dve.wait_ge(z.landed[w], it * (16 * WIN) + 16 * WIN * (NIT * g + 1))
                        if kind == SUM:
                            dve.wait_ge(z.squared, it * 2 + (2 * NIT * g + w + 1))
                        dve.wait_ge(z.stored[w], it * 16 + 16 * (1 + NIT * g))
                        for s in range(WIN):
                            done = it * (4 * WIN) + (SCAN0 + 4 * WIN * NIT * g + 2 * WIN * w + 2 * s - 1)
                            last = hist[:, w, s - 1, :] if s else hist[:, 1 - w, WIN - 1, :]
                            k = (it * 2 + w) * WIN + s
                            second = squares if kind == SUM else rows
                            dve.wait_ge(z.scan_ops, done)
                            v.scalar_tensor_tensor(hist[:, w, s, 0:F], last[:, 0:F], col[:, bass.ds(k, 1)],
                                                   rows[:, w, s, :], o0, o1).then_inc(z.scan_ops, 1)
                            dve.wait_ge(z.scan_ops, done + 1)
                            v.scalar_tensor_tensor(hist[:, w, s, F:2 * F], last[:, F:2 * F],
                                                   col[:, bass.ds(k, 1)], second[:, w, s, :], o0b, o2)\
                                .then_inc(z.scan_ops, 1)
                        v.tensor_copy(stage[:, w, :], idx[:, bass.ds((it * 2 + w + 2) * WIN, WIN)])\
                            .then_inc(z.staged, 1)
                dve.wait_ge(z.tail_turned, g + 1)
                for h, op in ((0, o1), (1, o2)):
                    m = 0 if kind == SUM else 1 + h
                    link(v.tensor_tensor_scan(cin[:, h, 1:P + 1], runm[:, m, :], turn[:, h, 0:P], 0.0,
                                              o0, op))
                dve.sem_inc(z.carry, 1)
                dve.wait_ge(z.carry_turned, g + 1)
                dve.wait_ge(z.first_in, 16 * (g + 1))
                for h, op in ((0, o1), (1, o2)):
                    link(v.tensor_tensor(fix[:, 1, h * F:(h + 1) * F], fix[:, 0, h * F:(h + 1) * F],
                                         turn[:, h, P:2 * P], op))
                dve.sem_inc(z.fixed, 1)

            general_asks = [0]
            link_base = [0]

            def general_sums(g, after):
                before = chain[0]
                chain[0] = 0
                link_sem[0] = general_chain[g]
                with dve.If(flagged(dve)):
                    if g > 1:
                        dve.wait_ge(main.ext_in, 16 * NT * (g - 1))
                        dve.sem_inc(spill_ready, 1)
                        dve.wait_ge(spilled, 16 * (2 * (g - 2) + 1))
                    for w in range(2):
                        dve.wait_ge(a_stored[w], 16 * (1 + (NT + 1 - w) // 2))
                    link(v.tensor_scalar(keep, neg[:], 0.0, None, ALU.is_equal))
                    scan(general, g, SUM)
                    dve.wait_ge(general.ext_in, 16 * NT * (g + 1))
                    link(v.tensor_copy(MEAN, EXT[:, :, 0:F]))
                    link(v.tensor_copy(STD, EXT[:, :, F:2 * F]))
                    if g > 1:
                        dve.sem_inc(unspill_ready, 1)
                        dve.wait_ge(spilled, 16 * (2 * (g - 2) + 2))
                    after()
                chain[0] = before
                link_sem[0] = dve_chain

            def evacuate(d, step):
                n, m = ITEMS[d], EVAC[d]
                dve.sem_inc(dense_in, 1)
                with dve.Fori(0, NG) as g:
                    dve.wait_ge(product, g * n + (ITEM_BASE[d] + n - d.startswith("post")))
                    step(g)
                dve.wait_ge(evac, EVAC_BASE[d] + NG * m)

            def tiles(t, g):
                return t[:].rearrange("p a f -> p (a f)")[:, bass.ds(g * (GT * F), GT * F)]\
                    .rearrange("p (a f) -> p a f", f=F)

            def add_bias(d, dest, bias):
                evacuate(d, lambda g: v.tensor_tensor(tiles(dest, g), acc[:, :, 0:F], over_n(bias, GT), ALU.add)
                         .then_inc(evac, 1))

            def layernorm(t):
                link(v.tensor_reduce(M0, t[:], AX.X, ALU.add))
                link(v.tensor_scalar(M0, M0, 1.0 / F, None, ALU.mult))
                link(v.tensor_tensor(t[:], t[:], over_f(M0), ALU.subtract))
                sq = EXT[:, :, 0:F]
                link(v.tensor_tensor(sq, t[:], t[:], ALU.mult))
                link(v.tensor_reduce(M1, sq, AX.X, ALU.add))
                link(v.tensor_scalar(M1, M1, 1.0 / F, EPS, ALU.mult, ALU.add))
                ask()
                link(v.reciprocal(M0, M2))
                link(v.tensor_tensor(t[:], t[:], over_f(M0), ALU.mult))

            general_sums(0, lambda: None)
            link(v.tensor_tensor(MEAN, MEAN, over_f(RDEG), ALU.mult))
            add_bias("sage0", H, V_B[0])
            link(v.tensor_scalar(H[:], H[:], 0.0, None, ALU.max))
            dve.sem_inc(table_ready, 1)
            parts(H[:], 0, Y[:])
            dve.sem_inc(parts_ready, 1)
            dve.wait_ge(sums_out, 2 * NT + 2)
            general_sums(1, lambda: None)
            link(v.tensor_tensor(MEAN, MEAN, over_f(RDEG), ALU.mult))
            add_bias("sage1", Y, V_B[1])
            link(v.tensor_tensor(X[:], X[:], Y[:], ALU.add))
            layernorm(X)

            for l, inp in ((0, X), (1, H)):
                d = f"pre{l}"

                def split(g):
                    v.tensor_tensor(tiles(C, g), acc[:, :, 0:F], over_n(V_BPRE[l], GT), ALU.add)\
                        .then_inc(evac, 1)
                    v.tensor_copy(tiles(Y, g), acc[:, :, F:2 * F]).then_inc(evac, 1)

                evacuate(d, split)
                dve.sem_inc(table_ready, 1)
                parts(Y[:], 0, MEAN)
                link(v.tensor_tensor(STD, Y[:], Y[:], ALU.mult))
                parts(STD, F, MEAN)
                dve.sem_inc(parts_ready, 1)
                scan(main, l, EXTREME)

                def statistics():
                    link(v.tensor_tensor(MEAN, MEAN, over_f(RDEG), ALU.mult))
                    link(v.tensor_tensor(STD, STD, over_f(RDEG), ALU.mult))
                    link(v.tensor_tensor(scratch, MEAN, MEAN, ALU.mult))
                    link(v.tensor_tensor(STD, STD, scratch, ALU.subtract))
                    link(v.tensor_scalar(STD, STD, 0.0, EPS, ALU.max, ALU.add))

                dve.wait_ge(sums_out, NT * (3 + l) + 2)
                statistics()
                ask()
                link(v.tensor_tensor(C[:], C[:], over_f(HAS), ALU.mult))
                link(v.tensor_tensor(MEAN, MEAN, C[:], ALU.add))

                def again():
                    statistics()
                    general_asks[0] += 1
                    dve.sem_inc(general_ask, 1)
                    dve.wait_ge(general_did, general_asks[0])
                    link(v.tensor_tensor(MEAN, MEAN, C[:], ALU.add))

                general_sums(2 + l, again)
                dve.wait_ge(main.ext_in, 16 * NT * (l + 1))
                for h, dest in ((0, Y), (1, C)):
                    link(v.tensor_tensor(EXT[:, :, h * F:(h + 1) * F], EXT[:, :, h * F:(h + 1) * F],
                                         over_f(HAS), ALU.mult))
                    link(v.tensor_tensor(dest[:], EXT[:, :, h * F:(h + 1) * F], C[:], ALU.add))
                d = f"post{l}"

                def finish(g):
                    u = tiles(STD, g)
                    v.tensor_tensor(u, acc[:, :, 0:F], over_n(V_BPOST[l], GT), ALU.add).then_inc(loop_chain, 1)
                    for j, scaler in ((1, AMP), (2, ATT)):
                        sc = scaler[:, bass.ds(g * GT, GT)].unsqueeze(2).to_broadcast([P, GT, F])
                        tmp = EXT[:, 0:GT, (j - 1) * F:j * F]
                        v.tensor_tensor(tmp, acc[:, :, j * F:(j + 1) * F], sc, ALU.mult).then_inc(loop_chain, 1)
                    n0 = 5 * NG * l
                    dve.wait_ge(loop_chain, g * 5 + (n0 + 3))
                    v.tensor_tensor(u, u, EXT[:, 0:GT, 0:F], ALU.add).then_inc(loop_chain, 1)
                    dve.wait_ge(loop_chain, g * 5 + (n0 + 4))
                    v.tensor_tensor(u, u, EXT[:, 0:GT, F:2 * F], ALU.add).then_inc(loop_chain, 1)
                    dve.wait_ge(loop_chain, g * 5 + (n0 + 5))
                    dve.sem_inc(u_ready, 1)
                    dve.sem_inc(evac, 1)
                    dve.wait_ge(product, g * ITEMS[d] + (ITEM_BASE[d] + ITEMS[d]))
                    v.tensor_tensor(tiles(Y, g), acc[:, :, 3 * F:4 * F], over_n(V_BLIN[l], GT), ALU.add)\
                        .then_inc(evac, 1)

                evacuate(d, finish)
                layernorm(Y)
                link(v.tensor_tensor(Y[:], Y[:], over_n(V_LNW[l]), ALU.mult))
                link(v.tensor_tensor(Y[:], Y[:], over_n(V_LNB[l]), ALU.add))
                if l == 0:
                    link(v.tensor_scalar(Y[:], Y[:], 0.0, None, ALU.max))
                    link(v.tensor_tensor(H[:], Y[:], X[:], ALU.add))
            link(v.tensor_tensor(Y[:], Y[:], H[:], ALU.add))
            link(v.tensor_tensor(Y[:], Y[:], X[:], ALU.add))
            layernorm(Y)
            dve.sem_inc(out_ready, 1)


_INS = ['x', 'src', 'dst', 'L0_gnn_W_self1', 'L0_gnn_W_neigh1', 'L0_gnn_b1', 'L0_gnn_W_self2', 'L0_gnn_W_neigh2',
        'L0_gnn_b2', 'L1_gnn_W_pre0', 'L1_gnn_b_pre0', 'L1_gnn_W_post0', 'L1_gnn_b_post0', 'L1_gnn_W_lin0',
        'L1_gnn_b_lin0', 'L1_gnn_ln_w0', 'L1_gnn_ln_b0', 'L1_gnn_W_pre1', 'L1_gnn_b_pre1', 'L1_gnn_W_post1',
        'L1_gnn_b_post1', 'L1_gnn_W_lin1', 'L1_gnn_b_lin1', 'L1_gnn_ln_w1', 'L1_gnn_ln_b1']


def kernel(**inputs):
    import numpy as np
    import concourse.bacc as bacc
    from concourse.bass_utils import run_bass_kernel_spmd

    nc = bacc.Bacc("TRN2", target_bir_lowering=False, num_devices=1)
    arrays, args = {}, []
    for name in _INS:
        a = np.ascontiguousarray(inputs[name])
        arrays[f"in_{name}"] = a
        args.append(nc.dram_tensor(f"in_{name}", a.shape, mybir.dt.from_np(a.dtype), kind="ExternalInput").ap())
    out = nc.dram_tensor("out", (N, F), F32, kind="ExternalOutput").ap()
    gnn_kernel(nc, *args, out)
    return run_bass_kernel_spmd(nc, [arrays], core_ids=[0]).results[0]["out"]
```

```python
import concourse.bass as bass
from concourse import mybir
from contextlib import ExitStack

F32 = mybir.dt.float32
I32 = mybir.dt.int32
BF16 = mybir.dt.bfloat16
F16 = mybir.dt.float16
ALU = mybir.AluOpType
ACT = mybir.ActivationFunctionType
AX = mybir.AxisListType

P = 128
F = 128
N = 3125
E = 100000
NT = -(-N // P)
LAST = N - (NT - 1) * P
WIN = 14
STEPS = 784
NIT = STEPS // (2 * WIN)
RUN_TAIL = E - (P - 1) * STEPS
SAMPLE = 200
NS = E // SAMPLE
NG = 5
GT = NT // NG
BATCHES = [range(0, NT // 2), range(NT // 2, NT)]
BIG = 3.0e38
OUT_OF_RANGE = 1.0e6
EPS = 1.0e-5
assert STEPS % (2 * WIN) == 0 and P * STEPS >= E and E % SAMPLE == 0 and NG * GT == NT

SLICE = 16
PER_BLOCK = P // SLICE
WT = 5
POOL_WT = 1
CODES = NT * SLICE
WINDOW = WT * P
MAX_COUNT = 250
REC_PAD = WINDOW
FLAG_FROM = 0.5
assert NT * PER_BLOCK * CODES < 2 ** 24

SUM, EXTREME = 0, 1
DENSE = ["sage0", "sage1", "pre0", "pre1"]
ITEMS = {"sage0": 2, "sage1": 2, "pre0": 1, "pre1": 1}
ITEM_BASE = {d: 1 + NG * sum(ITEMS[c] for c in DENSE[:i]) for i, d in enumerate(DENSE)}
EVAC = {"sage0": 1, "sage1": 1, "pre0": 2, "pre1": 2}
EVAC_BASE = {d: 1 + NG * sum(EVAC[c] for c in DENSE[:i]) for i, d in enumerate(DENSE)}


def first_root(l, g, later):
    return g + NG if l == 0 else 2 * NG + (g * 2 - 1 if later else 0)


def second_root(g):
    return g * 2 + (2 * NG + 2)


W_SAGE, W_PRE, W_LIN, W_POST = [0, 2], [4, 6], [8, 9], [10, 23]
NW = 36
V_B, V_BPRE, V_BPOST, V_BLIN, V_LNW, V_LNB = [0, 1], [2, 7], [3, 8], [4, 9], [5, 10], [6, 11]
NV = 12
SLOT = [0, 1, 2, 1, 2]
LAG = 2
OUT_LAG = 3
PRE = GT
assert GT == 5 and NT % 2 == 1 and NT // 2 + 1 <= NIT - NIT // 2
SCAN0 = 4 * WIN


def gnn_kernel(nc, x, src, dst, w_self1, w_neigh1, b1, w_self2, w_neigh2, b2,
               w_pre0, b_pre0, w_post0, b_post0, w_lin0, b_lin0, ln_w0, ln_b0,
               w_pre1, b_pre1, w_post1, b_post1, w_lin1, b_lin1, ln_w1, ln_b1, out):
    ctx = ExitStack()
    with ctx:
        def sb(name, shape, dt=F32):
            return ctx.enter_context(nc.sbuf_tensor(name, shape, dt))

        def sem(name):
            return ctx.enter_context(nc.semaphore(name))

        tables = [nc.dram_tensor(f"table{i}", [NT * P, F], F32).ap() for i in range(3)]
        history = nc.dram_tensor("history", [P * STEPS + 1, 2 * F], F32).ap()
        records = nc.dram_tensor("records", [(P * STEPS + REC_PAD) * 2], F32).ap()
        starts = nc.dram_tensor("starts", [2 * P], I32).ap()
        counts = nc.dram_tensor("counts", [NT, P, NT * P], BF16).ap()
        spill = nc.dram_tensor("spill", [P, NT * 2 * F], F32).ap()

        X = sb("X", [P, NT, F])
        H = sb("H", [P, NT, F])
        C = sb("C", [P, NT, F])
        Y = sb("Y", [P, NT, F])
        MS = sb("MS", [P, 2, NT, F])
        MEAN, STD = MS[:, 0], MS[:, 1]
        big = sb("big", [P, NT * 3 * F])
        XS = big[:].bitcast(BF16).rearrange("p (a c f) -> p a c f", c=3, f=2 * F)
        EXT = big[:, 0:NT * 2 * F].rearrange("p (a f) -> p a f", f=2 * F)
        A = sb("A", [P, 2, NT, P], BF16)
        rows = sb("rows", [P, 2, WIN, F])
        rowsf = rows[:].rearrange("p w s f -> p (w s f)")
        hist = sb("hist", [P, 2, WIN, 2 * F])
        histf = hist[:].rearrange("p w s f -> p (w s f)")
        idx = sb("idx", [P, STEPS + 2 * WIN], I32)
        stage = sb("stage", [P, 2, WIN], I32)
        neg = sb("neg", [P, STEPS])
        weights = sb("weights", [P, NW, F])
        vectors = sb("vectors", [P, NV, F])
        ident = sb("ident", [P, P])
        ones = sb("ones", [P, P])
        runm = sb("runm", [P, 3, P])
        cin = sb("cin", [P, 2, P + 1])
        fix = sb("fix", [P, 2, 2 * F])
        small = sb("small", [P, 16, NT])
        tiny = sb("tiny", [P, 32])
        stats = sb("stats", [P, 2, GT, 2])
        icol = sb("icol", [P, 3, NT], I32)
        fixI = sb("fixI", [P, 1], I32)
        flagI = sb("flagI", [1, 1], I32)
        lhs = rowsf[:, 0:2 * GT * P].rearrange("p (a b) -> p a b", a=2)
        lhs_ext = rowsf[:, 0:3 * 2 * P].rearrange("p (a b) -> p a b", a=3)
        lhs_u = rowsf[:, 6 * P:9 * P].rearrange("p (a b) -> p a b", a=3)
        staged = rowsf[:, 10 * P:10 * P + GT * F].rearrange("p (t f) -> p t f", f=F)
        o = 10 * P + GT * F
        bn = rowsf[:, o:o + 2 * GT * 6].rearrange("p (t c) -> p t c", c=6)
        squares = MS[:].rearrange("p m a f -> p (m a f)")[:, 0:2 * WIN * F]\
            .rearrange("p (w s f) -> p w s f", w=2, s=WIN)
        keep = A[:].rearrange("p s a d -> p (s a d)").bitcast(F32)[:, 0:STEPS]
        af = A[:].rearrange("p s a d -> p (s a d)").bitcast(F32)
        operands = af[:, STEPS:STEPS + 4 * F].rearrange("p (q f) -> p q f", q=4)
        operandsT = af[:, STEPS + 4 * F:STEPS + 8 * F].rearrange("p (q f) -> p q f", q=4)
        ONE = WT * 2
        hot_s = histf[:, 0:ONE * P // 2].bitcast(BF16).rearrange("p (h c t) -> p h c t", h=2, t=WT)
        o = ONE * P // 2
        hot_c = histf[:, o:o + ONE * CODES // 2].bitcast(BF16).rearrange("p (t c) -> p t c", c=CODES)
        o += ONE * CODES // 2
        win = histf[:, o:o + PER_BLOCK * WT * 2].rearrange("p (j t c) -> p j t c", j=PER_BLOCK, c=2)
        o += PER_BLOCK * WT * 2
        codes = histf[:, o:o + PER_BLOCK * WT].rearrange("p (j t) -> p j t", j=PER_BLOCK)
        o += PER_BLOCK * WT
        lows = histf[:, o:o + PER_BLOCK * WT // 2].bitcast(F16).rearrange("p (j t) -> p j t", j=PER_BLOCK)
        o += PER_BLOCK * WT // 2
        iota_s = histf[:, o:o + P * WT // 2].bitcast(F16).rearrange("p (c t) -> p c t", t=WT)
        o += P * WT // 2
        slice_base = histf[:, o:o + 2 * P]
        o += 2 * P
        iota_c = histf[:, o:o + CODES // 2].bitcast(F16)
        o += CODES // 2
        startrow = histf.bitcast(I32)[0:1, o:o + 2 * P]
        o += 2 * P
        assert o <= 2 * WIN * 2 * F
        hf, cf, yf = (t[:].rearrange("p a b -> p (a b)") for t in (H, C, Y))
        msf = MS[:].rearrange("p m a f -> p (m a f)")
        dstI = hf.bitcast(I32)[:, 0:STEPS + 2]
        ints1 = hf.bitcast(I32)[:, STEPS + 8:2 * STEPS + 8]
        kposI = hf.bitcast(I32)[:, 2 * STEPS + 16:3 * STEPS + 16]
        dstF = cf[:, 0:STEPS + 2]
        restart = cf[:, STEPS + 2:2 * STEPS + 2]
        ends = cf[:, 2 * STEPS + 2:3 * STEPS + 2]
        kpos = cf[:, 3 * STEPS + 2:4 * STEPS + 2]
        shift = rowsf[:, 0:P]
        wrap = rowsf[:, P:2 * P]
        jcodeI = rowsf.bitcast(I32)[:, 2 * P:2 * P + CODES]
        jsliceI = rowsf.bitcast(I32)[:, 2 * P + CODES:4 * P + CODES]
        limitI = rowsf.bitcast(I32)[:, 4 * P + CODES:4 * P + CODES + 4]
        sampI = msf.bitcast(I32)[0:1, 0:NS]
        sampF = msf[0:1, NS:2 * NS]
        samples = msf[:, 2 * NS:3 * NS]
        rec = msf[:, 3 * NS:3 * NS + 2 * STEPS].rearrange("p (k c) -> p k c", c=2)
        o = 3 * NS + 2 * STEPS
        wchunks = msf.bitcast(I32)[:, o:o + 4 * SAMPLE].rearrange("p (j k) -> p j k", k=SAMPLE)
        wjunk = yf[:, 0:4 * NS].rearrange("p (j k) -> p j k", k=NS)
        wjunk2 = yf[:, 0:4 * SAMPLE].rearrange("p (j k) -> p j k", k=SAMPLE)
        recpad = yf[:, 4 * NS:4 * NS + 2 * WT]
        signs_out = yf[:, NT * F - 2 * NS:].rearrange("p (h k) -> p h k", h=2)
        ai, per_slot = A[:].rearrange("p s a d -> p (s a d)").bitcast(I32), NT * P // 2
        in_a = (per_slot - P // 2) // SAMPLE
        chunks = [ai[:, o:o + SAMPLE] for o in
                  [w * per_slot + P // 2 + i * SAMPLE for w in range(2) for i in range(in_a)]]
        chunks += [histf.bitcast(I32)[:, i * SAMPLE:(i + 1) * SAMPLE] for i in range(NT - 2 * in_a)]
        assert (NT - 2 * in_a) * SAMPLE <= ONE * (P + CODES) // 2
        nodeI, chunkI, endI = (icol[:, i, :] for i in range(3))
        wchunkI = fix[:, 1, 0:4].bitcast(I32)
        wstartI = fix[:, 1, 4:6].bitcast(I32)
        (NODE, CNT, CHUNK, LE, LT, HAS, DEGC, RDEG, LOGD, AMP, ATT, M0, M1, M2, LOG1, RSTD) = \
            [small[:, i, :] for i in range(16)]
        scales, shifts, negmean = (RSTD[:, i * GT:(i + 1) * GT] for i in range(3))
        rstd = RSTD[:, 3 * GT:4 * GT]

        acc = ctx.enter_context(nc.psum_tensor("acc", [P, GT, 512], F32))
        turn = ctx.enter_context(nc.psum_tensor("turn", [P, 2, 512], F32))
        turnf = turn[:].rearrange("p a b -> p (a b)")
        turn_u = ctx.enter_context(nc.psum_tensor("turn_u", [P, 512], F32))

        consts = sem("consts")
        pool_chain = sem("pool_chain")
        x_in = sem("x_in")
        dst_in = sem("dst_in")
        src_in = sem("src_in")
        weights_in = sem("weights_in")
        padded = sem("padded")
        dve_chain = sem("dve_chain")
        small_mm = sem("small_mm")
        pe_go = sem("pe_go")
        wchunk_ready = sem("wchunk_ready")
        wchunks_in = sem("wchunks_in")
        chunk_ready = sem("chunk_ready")
        chunks_in = [sem("chunks_in0"), sem("chunks_in1")]
        starts_ready = sem("starts_ready")
        starts_out = sem("starts_out")
        starts_in = sem("starts_in")
        rec_ready = sem("rec_ready")
        rec_out = sem("rec_out")
        flag_ready = sem("flag_ready")
        act_ask = sem("act_ask")
        act_did = sem("act_did")
        table_ready = sem("table_ready")
        table_in = sem("table_in")
        table_done = sem("table_done")
        win_in = [sem(f"win_in{j}") for j in range(PER_BLOCK)]
        windows_read = sem("windows_read")
        onehots = sem("onehots")
        onehots_pool = sem("onehots_pool")
        slice_opened = sem("slice_opened")
        tallied = sem("tallied")
        counted = sem("counted")
        a_stored = [sem("a_stored0"), sem("a_stored1")]
        a_in = [sem("a_in0"), sem("a_in1")]
        parts_ready = sem("parts_ready")
        summed = sem("summed")
        sums_out = sem("sums_out")

        class ScanSems:
            def __init__(self, name):
                self.staged = sem(name + "staged")
                self.window_opened = sem(name + "window_opened")
                self.landed = [sem(name + "landed0"), sem(name + "landed1")]
                self.scan_ops = sem(name + "scan_ops")
                self.squared = sem(name + "squared")
                self.stored = [sem(name + "stored0"), sem(name + "stored1")]
                self.tail_turned = sem(name + "tail_turned")
                self.carry = sem(name + "carry")
                self.carry_turned = sem(name + "carry_turned")
                self.first_in = sem(name + "first_in")
                self.fixed = sem(name + "fixed")
                self.fix_out = sem(name + "fix_out")
                self.ext_in = [sem(name + f"ext_in{i}") for i in range(NG)]
                self.means = sem(name + "means")
                self.varied = sem(name + "varied")
                self.rooted = sem(name + "rooted")
                self.part_turned = sem(name + "part_turned")
                self.part_copied = sem(name + "part_copied")
                self.part_product = sem(name + "part_product")
                self.sums_in = sem(name + "sums_in")
                self.partial = sem(name + "partial")
                self.combined = sem(name + "combined")
                self.start = sem(name + "start")

        main = ScanSems("x_")
        general = ScanSems("g_")
        general_chain = [sem(f"general_chain{g}") for g in range(4)]
        zeroed = sem("zeroed")
        spill_ready = sem("spill_ready")
        spilled = sem("spilled")
        unspill_ready = sem("unspill_ready")
        dense_in = sem("dense_in")
        zero_row = sem("zero_row")
        signs = sem("signs")
        parts_chain = sem("parts_chain")
        post_chain = [sem("post_chain0"), sem("post_chain1")]
        ext_turned = sem("ext_turned")
        ext_copied = sem("ext_copied")
        ext_product = sem("ext_product")
        u_ready = sem("u_ready")
        lin_turned = sem("lin_turned")
        lin_copied = sem("lin_copied")
        lin_product = sem("lin_product")
        lin_out = sem("lin_out")
        bn_ready = sem("bn_ready")
        root_ask = sem("root_ask")
        root_did = sem("root_did")
        x1_ready = sem("x1_ready")
        hidden_chain = sem("hidden_chain")
        result_chain = sem("result_chain")
        h_ready = sem("h_ready")
        rows_ready = sem("rows_ready")
        turned = sem("turned")
        copied = sem("copied")
        product = sem("product")
        evac = sem("evac")
        scales_ready = sem("scales_ready")
        normed = sem("normed")
        out_ready = sem("out_ready")
        out_stored = sem("out_stored")

        def flagged(eng):
            eng.wait_ge(flag_ready, 1)
            return eng.value_load(flagI[0:1, 0:1], min_val=0, max_val=1)

        block = ctx.enter_context(nc.Block())

        @block.sync
        def _(sp):
            sp.wait_ge(padded, 1)
            runs = dst[0:(P - 1) * STEPS].rearrange("(p k) -> p k", k=STEPS)
            with nc.allow_non_contiguous_dma(reason="one value for each partition"):
                sp.dma_start(sampI, dst.rearrange("(a s k) -> a s k", a=1, k=SAMPLE)[:, :, 0])\
                    .then_inc(dst_in, 16)
                sp.dma_start(dstI[0:P - 1, 1:STEPS + 1], runs).then_inc(dst_in, 16)
                sp.dma_start(dstI[P - 1:P, 1:RUN_TAIL + 1],
                             dst[(P - 1) * STEPS:E].rearrange("(a k) -> a k", a=1)).then_inc(dst_in, 16)
                sp.dma_start(dstI[1:P, 0:1], runs[:, STEPS - 1:STEPS]).then_inc(dst_in, 16)
                sp.dma_start(dstI[0:P - 2, STEPS + 1:STEPS + 2], runs[1:P - 1, 0:1]).then_inc(dst_in, 16)
                sp.dma_start(dstI[P - 2:P - 1, STEPS + 1:STEPS + 2],
                             dst[(P - 1) * STEPS:(P - 1) * STEPS + 1].rearrange("(a k) -> a k", a=1))\
                    .then_inc(dst_in, 16)
            sp.dma_start(idx[0:P - 1, 0:STEPS],
                         src[0:(P - 1) * STEPS].rearrange("(p k) -> p k", k=STEPS)).then_inc(src_in, 16)
            sp.dma_start(idx[P - 1:P, 0:RUN_TAIL],
                         src[(P - 1) * STEPS:E].rearrange("(a k) -> a k", a=1)).then_inc(src_in, 16)
            sp.dma_start(X[:, 0:NT - 1, :], x[0:(NT - 1) * P, :].rearrange("(b p) f -> p b f", p=P))\
                .then_inc(x_in, 16)
            sp.dma_start(X[0:LAST, NT - 1, :], x[(NT - 1) * P:N, :]).then_inc(x_in, 16)
            sp.wait_ge(rec_ready, 1)
            sp.dma_start(records[0:P * STEPS * 2].rearrange("(p q) -> p q", p=P),
                         rec.rearrange("p k c -> p (k c)")).then_inc(rec_out, 16)
            sp.dma_start(records[P * STEPS * 2:].rearrange("(p q) -> p q", p=P), recpad).then_inc(rec_out, 16)
            sp.wait_ge(starts_ready, 1)
            with nc.allow_non_contiguous_dma(reason="one value for each slice"):
                sp.dma_start(starts.rearrange("(t p) -> p t", p=P), wstartI).then_inc(starts_out, 16)
            sp.wait_ge(starts_out, 16)
            sp.dma_start(startrow, starts.rearrange("(a k) -> a k", a=1)).then_inc(starts_in, 16)
            sp.dma_start(history[P * STEPS:P * STEPS + 1, :], fix[0:1, 0, :]).then_inc(zero_row, 16)
            sp.wait_ge(zero_row, 16)
            for sems in (main, general):
                for w in range(2):
                    sp.dma_start(history[0:P, 0:P], ident[:]).then_inc(sems.stored[w], 16)
                    sp.wait_ge(sems.stored[w], 16)
            sp.wait_ge(rec_out, 32)
            sp.wait_ge(starts_in, 16)
            with sp.Fori(0, NT) as b:
                sp.wait_ge(windows_read, b * 2 + 2)
                for j in range(PER_BLOCK):
                    e = sp.value_load(startrow[0:1, bass.ds(b * PER_BLOCK + j, 1)], min_val=0, max_val=E)
                    sp.dma_start(win[:, j].rearrange("p t c -> p (t c)"),
                                 records[bass.ds(e * 2, WINDOW * 2)].rearrange("(p q) -> p q", p=P))\
                        .then_inc(win_in[j], 16)

            hist_v = history[0:P * STEPS].rearrange("(p k) f -> p (k f)", k=STEPS)

            def store_history(z, g):
                sp.wait_ge(z.start, g + 1)
                with sp.Fori(0, NIT) as it:
                    for w in range(2):
                        for part in range(2):
                            sp.wait_ge(z.scan_ops, it * (4 * WIN) +
                                       (SCAN0 + 2 * WIN * (2 * NIT * g + w) + WIN * (part + 1)))
                            sp.dma_start(hist_v[:, bass.ds((it * 4 + w * 2 + part) * (WIN * F), WIN * F)],
                                         histf[:, (w * 2 + part) * WIN * F:(w * 2 + part + 1) * WIN * F])\
                                .then_inc(z.stored[w], 16)

            def general_sums(g):
                with sp.If(flagged(sp)):
                    if g == 1:
                        sp.wait_ge(table_ready, 1)
                        sp.dma_start(tables[0].rearrange("(b p) f -> p b f", p=P), H[:]).then_inc(table_in, 16)
                    if g > 1:
                        sp.wait_ge(spill_ready, g - 1)
                        sp.dma_start(spill, EXT.rearrange("p a f -> p (a f)")).then_inc(spilled, 16)
                    store_history(general, g)
                    if g > 1:
                        sp.wait_ge(unspill_ready, g - 1)
                        sp.dma_start(EXT.rearrange("p a f -> p (a f)"), spill).then_inc(spilled, 16)

            general_sums(0)
            general_sums(1)
            for l in range(2):
                for g in range(NG):
                    sp.wait_ge(rows_ready, NG * l + g + 1)
                    sp.dma_start(tables[1 + l].rearrange("(b p) f -> p b f", p=P)[:, g * GT:(g + 1) * GT],
                                 Y[:, g * GT:(g + 1) * GT]).then_inc(table_done, 16)
                store_history(main, l)
                general_sums(2 + l)
            for g in range(NG):
                sp.wait_ge(out_ready, g + 1)
                last = min((g + 1) * GT, NT - 1)
                sp.dma_start(out[g * GT * P:last * P, :].rearrange("(b p) f -> p b f", p=P),
                             Y[:, g * GT:last, :]).then_inc(out_stored, 16)
            sp.dma_start(out[(NT - 1) * P:N, :], Y[0:LAST, NT - 1, :]).then_inc(out_stored, 16)
            sp.wait_ge(out_stored, 16 * (NG + 1))

        @block.scalar
        def _(act):
            for w, at in ((w_self1, 0), (w_neigh1, 1), (w_self2, 2), (w_neigh2, 3), (w_lin0, 8), (w_lin1, 9)):
                act.dma_start(weights[:, at, :], w).then_inc(weights_in, 16)
            for l, w in enumerate((w_pre0, w_pre1)):
                act.dma_start(weights[:, W_PRE[l]:W_PRE[l] + 2, :], w.rearrange("(a p) f -> p a f", p=P))\
                    .then_inc(weights_in, 16)
            for l, w in enumerate((w_post0, w_post1)):
                at = W_POST[l]
                act.dma_start(weights[:, at, :], w[0:F, :]).then_inc(weights_in, 16)
                for j in range(3):
                    act.dma_start(weights[:, at + 1 + j:at + 11 + j:3, :],
                                  w[(1 + 4 * j) * F:(5 + 4 * j) * F, :].rearrange("(a p) f -> p a f", p=P))\
                        .then_inc(weights_in, 16)
            for i, v in enumerate((b1, b2, b_pre0, b_post0, b_lin0, ln_w0, ln_b0, b_pre1, b_post1, b_lin1,
                                   ln_w1, ln_b1)):
                act.dma_start(vectors[:, i, :], v.partition_broadcast(P)).then_inc(weights_in, 16)
            asked = [0]

            done = [0]

            def count_up_to(values, n, tiles):
                asked[0] += 1
                act.wait_ge(act_ask, asked[0])
                for b in tiles:
                    if done[0] > 1:
                        act.wait_ge(signs, done[0] - 1)
                    nc.scalar.activation(signs_out[:, done[0] % 2, 0:n], values(b), ACT.Sign,
                                         bias=LT[:, b:b + 1], scale=-1.0, accum_out=CNT[:, b:b + 1])\
                        .then_inc(signs, 1)
                    done[0] += 1
                act.wait_ge(signs, done[0])
                act.sem_inc(act_did, 1)

            for tiles in BATCHES:
                count_up_to(lambda b: samples, NS, tiles)
            for i, tiles in enumerate(BATCHES):
                act.wait_ge(chunks_in[i], 16 * len(tiles))
                count_up_to(lambda b: chunks[b], SAMPLE, tiles)

            act.sem_inc(copied, 1)
            act.sem_inc(counted, 2)
            act.sem_inc(sums_out, 2)
            act.sem_inc(ext_copied, PRE)
            act.sem_inc(lin_copied, PRE)
            act.wait_ge(zeroed, 1)
            for w in range(2):
                act.dma_start(counts[0, :, 0:P], A[:, w, 0, :]).then_inc(a_stored[w], 16)
                act.wait_ge(a_stored[w], 16)

            def function(o, i, func):
                asked[0] += 1
                act.wait_ge(act_ask, asked[0])
                nc.scalar.activation(o, i, func).then_inc(act_did, 1)

            def take_sums(k, b, bank, width):
                act.wait_ge(summed, b + (NT * k + 3))
                if width == F:
                    nc.scalar.activation(msf[:, bass.ds(b * F, F)], acc[:, bank, 0:F], ACT.Copy,
                                         scale=RDEG[:, bass.ds(b, 1)]).then_inc(sums_out, 1)
                else:
                    nc.scalar.copy(msf[:, bass.ds(b * F, F)], acc[:, bank, 0:F])
                    nc.scalar.copy(msf[:, bass.ds(b * F + NT * F, F)], acc[:, bank, F:2 * F])\
                        .then_inc(sums_out, 1)

            def make_block(b, slot, first=False):
                act.wait_ge(summed, b + 1)
                act.wait_ge(a_stored[slot], (b - slot) * 8 + 16)
                for j in range(PER_BLOCK):
                    act.wait_ge(tallied, b * PER_BLOCK + (j + 3))
                    nc.scalar.copy(A[:, slot, :, j * SLICE:(j + 1) * SLICE],
                                   acc[:, j % 2, 0:CODES].rearrange("p (a d) -> p a d", d=SLICE))\
                        .then_inc(counted, 1)
                act.wait_ge(counted, b * PER_BLOCK + (PER_BLOCK + 2))
                act.dma_start(counts_v[:, bass.ds(b, 1), :].rearrange("p b q -> p (b q)"),
                              A[:, slot].rearrange("p a d -> p (a d)")).then_inc(a_stored[slot], 16)
                if not first:
                    take_sums(0, b - 1, 2 + 1 - slot, F)

            def load_block(b, slot):
                act.dma_start(A[:, slot].rearrange("p a d -> p (a d)"),
                              counts_v[:, bass.ds(b, 1), :].rearrange("p b q -> p (b q)")).then_inc(a_in[slot], 16)

            def sums(k, width):
                act.wait_ge(parts_ready, k + 1)
                load_block(0, 0)
                load_block(1, 1)
                with act.Fori(0, NT // 2 - 1) as i:
                    for s in range(2):
                        take_sums(k, i * 2 + s, s, width)
                        load_block(i * 2 + (s + 2), s)
                take_sums(k, NT - 3, 0, width)
                load_block(NT - 1, 0)
                take_sums(k, NT - 2, 1, width)
                take_sums(k, NT - 1, 0, width)

            def root(group):
                act.wait_ge(root_ask, group + 1)
                nc.scalar.activation(M2[:, 0:GT], M1[:, 0:GT], ACT.Sqrt).then_inc(root_did, 1)

            def lhs_copies(d, g):
                n = ITEMS[d]
                for q in range(n):
                    act.wait_ge(turned, g * n + (ITEM_BASE[d] + q))
                    act.wait_ge(product, g * n + (ITEM_BASE[d] + max(q - 1, 0)))
                    nc.scalar.copy(lhs[:, q % 2, :], turnf[:, 0:GT * P]).then_inc(copied, 1)

            def dense(d):
                with act.Fori(0, NG) as g:
                    lhs_copies(d, g)

            def squares_of(z, g):
                with act.Fori(0, NIT) as it:
                    for w in range(2):
                        act.wait_ge(z.landed[w], it * (16 * WIN) + 16 * WIN * (NIT * g + 1))
                        act.wait_ge(z.scan_ops, it * (4 * WIN) + (SCAN0 + 2 * WIN * (2 * NIT * g + w - 1)))
                        nc.scalar.activation(squares[:, w].rearrange("p s f -> p (s f)"),
                                             rows[:, w].rearrange("p s f -> p (s f)"), ACT.Square)\
                            .then_inc(z.squared, 1)

            def tile(t, b):
                return t.rearrange("p a f -> p (a f)")[:, bass.ds(b * F, F)]

            def partials(z, l):
                if l == 0:
                    act.sem_inc(z.part_copied, 1)
                with act.Fori(0, NT) as b:
                    act.wait_ge(z.part_turned, b + (NT * l + 1))
                    rdeg = RDEG[:, bass.ds(b, 1)]
                    nc.scalar.activation(operands[:, 0], tile(MEAN, b), ACT.Copy, scale=rdeg)
                    nc.scalar.activation(operands[:, 2], tile(MEAN, b), ACT.Square, scale=rdeg)
                    nc.scalar.activation(operands[:, 1], tile(C[:], b), ACT.Copy, scale=HAS[:, bass.ds(b, 1)])
                    nc.scalar.copy(operands[:, 3], tile((X, H)[l][:], b)).then_inc(z.means, 1)
                    act.wait_ge(z.varied, b * 2 + (NT * 2 * l + 2))
                    nc.scalar.activation(operands[:, 2], operands[:, 2], ACT.Sqrt).then_inc(z.rooted, 1)
                    act.wait_ge(z.part_turned, b + (NT * l + 2))
                    act.wait_ge(z.part_product, b + (NT * l + 1))
                    nc.scalar.copy(operandsT.rearrange("p q f -> p (q f)"), acc[:, 3, :])\
                        .then_inc(z.part_copied, 1)

            def general_sums(g):
                with act.If(flagged(act)):
                    squares_of(general, g)
                    if g > 1:
                        act.wait_ge(general.sums_in, g - 1)
                        partials(general, g - 2)

            def post(l):
                def copy_u(b, t):
                    act.wait_ge(lin_turned, b + (NT * l + 1))
                    act.wait_ge(lin_product, b + (NT * l - 1 + PRE))
                    nc.scalar.copy(lhs_u[:, SLOT[t % GT], :], turn_u[:, 0:P]).then_inc(lin_copied, 1)

                def normalise(g, first, last):
                    act.wait_ge(scales_ready, g + (NG * l + 1))
                    for t in range(first, last + 1):
                        y = tile(Y[:], g * GT + t)
                        nc.scalar.activation(y, y, ACT.Identity, bias=shifts[:, t:t + 1],
                                             scale=scales[:, t:t + 1]).then_inc(normed, 1)

                def group(g, prev, prev2):
                    for t in range(GT):
                        b = g * GT + t
                        act.wait_ge(ext_turned, b + (NT * l + 1))
                        act.wait_ge(ext_product, b + (NT * l - 1 + PRE))
                        nc.scalar.copy(lhs_ext[:, SLOT[t], :], turn[:, t % 2, 0:2 * P])\
                            .then_inc(ext_copied, 1)
                        if t == OUT_LAG and prev:
                            root(first_root(l, g - 1, prev2))
                        if t == OUT_LAG + 1 and prev2 and l == 1:
                            root(second_root(g - 2))
                        if t >= LAG or prev:
                            copy_u(b - LAG, t - LAG)
                        if t == GT - 1 and prev:
                            normalise(g - 1, 0, 1)
                        if t == 0 and prev2:
                            normalise(g - 2, 2, 3)
                        if t == 1 and prev2:
                            normalise(g - 2, 4, 4)

                group(0, False, False)
                group(1, True, False)
                with act.Fori(2, NG) as g:
                    group(g, True, True)
                copy_u(NT - 2, GT - 2)
                normalise(NG - 2, 2, 3)
                copy_u(NT - 1, GT - 1)
                normalise(NG - 2, 4, 4)
                root(first_root(l, NG - 1, True))
                if l == 1:
                    root(second_root(NG - 2))
                normalise(NG - 1, 0, GT - 1)
                if l == 1:
                    root(second_root(NG - 1) - 1)

            counts_v = counts.rearrange("b p q -> p b q")
            function(LOGD, DEGC, ACT.Ln)
            function(LOG1, M0, ACT.Ln)
            nc.scalar.activation(M2[:, GT:GT + 1], DEGC[:, 0:1], ACT.Sqrt)
            make_block(0, 0, first=True)
            with act.Fori(0, NT // 2) as i:
                make_block(i * 2 + 1, 1)
                make_block(i * 2 + 2, 0)
            take_sums(0, NT - 1, 2, F)
            for w in range(2):
                act.wait_ge(a_stored[w], 16 * (1 + (NT + 1 - w) // 2))
            general_sums(0)
            dense("sage0")
            sums(1, F)
            general_sums(1)
            lhs_copies("sage1", 0)
            with act.Fori(1, NG) as g:
                lhs_copies("sage1", g)
                root(g - 1)
            root(NG - 1)
            for l in range(2):
                dense(f"pre{l}")
                sums(2 + l, 2 * F)
                partials(main, l)
                general_sums(2 + l)
                post(l)

        @block.gpsimd
        def _(pool):
            nc.gpsimd.memset(ident[:], 0.0).then_inc(pool_chain, 1)
            nc.gpsimd.memset(shift, 0.0).then_inc(pool_chain, 1)
            nc.gpsimd.memset(wrap, 0.0).then_inc(pool_chain, 1)
            nc.gpsimd.memset(ones[:], 1.0).then_inc(consts, 1)
            nc.gpsimd.iota(limitI.rearrange("p (a t) -> p a t", a=2), pattern=[[SLICE, 2], [SLICE * P, 2]],
                           base=0, channel_multiplier=SLICE).then_inc(consts, 1)
            nc.gpsimd.iota(nodeI, pattern=[[P, NT]], base=0, channel_multiplier=1).then_inc(consts, 1)
            nc.gpsimd.iota(kposI, pattern=[[1, STEPS]], base=0, channel_multiplier=0).then_inc(consts, 1)
            nc.gpsimd.iota(jcodeI, pattern=[[1, CODES]], base=0, channel_multiplier=0).then_inc(consts, 1)
            nc.gpsimd.iota(jsliceI, pattern=[[CODES, 2 * P]], base=0, channel_multiplier=0).then_inc(consts, 1)
            pool.wait_ge(pool_chain, 3)
            nc.gpsimd.affine_select(out=ident[:], in_=ident[:], compare_op=ALU.not_equal, fill=1.0,
                                    base=0, pattern=[[-1, P]], channel_multiplier=1).then_inc(consts, 1)
            nc.gpsimd.affine_select(out=shift, in_=shift, compare_op=ALU.not_equal, fill=1.0,
                                    base=1, pattern=[[-1, P]], channel_multiplier=1).then_inc(consts, 1)
            nc.gpsimd.affine_select(out=wrap, in_=wrap, compare_op=ALU.not_equal, fill=1.0,
                                    base=-(P - 1), pattern=[[P, P]], channel_multiplier=1)\
                .then_inc(consts, 1)
            by_chunk = dst.rearrange("(s k) -> s k", k=SAMPLE)
            pool.wait_ge(wchunk_ready, 1)
            for t in range(4):
                nc.gpsimd.indirect_dma_start(
                    out=wchunks[:, t, :], out_offset=None, in_=by_chunk,
                    in_offset=bass.IndirectOffsetOnAxis(ap=wchunkI[:, t:t + 1], axis=0)).then_inc(wchunks_in, 16)
            for i, tiles in enumerate(BATCHES):
                pool.wait_ge(chunk_ready, i + 1)
                for b in tiles:
                    nc.gpsimd.indirect_dma_start(
                        out=chunks[b], out_offset=None, in_=by_chunk,
                        in_offset=bass.IndirectOffsetOnAxis(ap=chunkI[:, b:b + 1], axis=0))\
                        .then_inc(chunks_in[i], 16)

            pool.sem_inc(onehots_pool, 1)
            pool.wait_ge(parts_ready, 1)
            with pool.Fori(0, NT) as b:
                pool.wait_ge(windows_read, b * 2 + 4)
                for j in range(PER_BLOCK):
                    pool.wait_ge(tallied, b * PER_BLOCK + (j + 1))
                    pool.sem_inc(slice_opened, 1)
                    for t in range(WT - POOL_WT, WT):
                        m = nc.gpsimd.tensor_scalar(hot_c[:, (j % 2) * WT + t, :], iota_c, codes[:, j, t:t + 1],
                                                    None, ALU.is_equal)
                    m.then_inc(onehots_pool, 1)

            def gather(z, g, table):
                pool.wait_ge(z.start, g + 1)
                with pool.Fori(0, NIT) as it:
                    for w in range(2):
                        pool.wait_ge(z.staged, it * 2 + (2 * (NIT + 1) * g + w + 1))
                        pool.sem_inc(z.window_opened, 1)
                        for s in range(WIN):
                            nc.gpsimd.indirect_dma_start(
                                out=rows[:, w, s, :], out_offset=None, in_=table,
                                in_offset=bass.IndirectOffsetOnAxis(ap=stage[:, w, s:s + 1], axis=0))\
                                .then_inc(z.landed[w], 16)
                for w in range(2):
                    pool.wait_ge(z.stored[w], 16 * (1 + 2 * NIT * (g + 1)))
                nc.gpsimd.indirect_dma_start(
                    out=fix[:, 0, :], out_offset=None, in_=history,
                    in_offset=bass.IndirectOffsetOnAxis(ap=fixI[:, 0:1], axis=0),
                    bounds_check=P * STEPS - 1, oob_is_err=False).then_inc(z.first_in, 16)
                pool.wait_ge(z.fixed, g + 1)
                nc.gpsimd.indirect_dma_start(
                    out=history, out_offset=bass.IndirectOffsetOnAxis(ap=fixI[:, 0:1], axis=0),
                    in_=fix[:, 1, :], in_offset=None,
                    bounds_check=P * STEPS - 1, oob_is_err=False).then_inc(z.fix_out, 16)
                pool.wait_ge(z.fix_out, 16 * (g + 1))
                for b in range(NT):
                    nc.gpsimd.indirect_dma_start(
                        out=EXT[:, b, :], out_offset=None, in_=history,
                        in_offset=bass.IndirectOffsetOnAxis(ap=endI[:, b:b + 1], axis=0))\
                        .then_inc(z.ext_in[b // GT], 16)

            def general_sums(g):
                with pool.If(flagged(pool)):
                    if g == 1:
                        pool.wait_ge(table_in, 16)
                    gather(general, g, (x, tables[0], tables[1], tables[2])[g])

            general_sums(0)
            general_sums(1)
            for l in range(2):
                pool.wait_ge(table_done, 16 * NG * (1 + l))
                gather(main, l, tables[1 + l])
                general_sums(2 + l)

        @block.tensor
        def _(pe):
            pe.sem_inc(product, 1)
            pe.sem_inc(tallied, 2)
            pe.sem_inc(summed, 2)
            pe.sem_inc(ext_product, PRE)
            pe.sem_inc(lin_product, PRE)
            pe.wait_ge(consts, 9)
            pe.wait_ge(pe_go, 1)
            nc.tensor.matmul(acc[:, 0, 0:NS], ones[0:1, :], sampF, start=True, stop=True).then_inc(small_mm, 1)
            pe.wait_ge(pe_go, 2)
            nc.tensor.matmul(acc[:, 3, 0:P], tiny[:, 4:5].to_broadcast([P, P]), ident[:],
                             start=True, stop=True).then_inc(small_mm, 1)
            pe.wait_ge(pe_go, 3)
            nc.tensor.matmul(acc[:, 1, 0:NT], shift, LE, start=True, stop=False)
            nc.tensor.matmul(acc[:, 1, 1:NT], wrap, LE[:, 0:NT - 1], start=False, stop=True)\
                .then_inc(small_mm, 1)
            pe.wait_ge(pe_go, 4)
            nc.tensor.matmul(acc[:, 2, 0:2], ones[:], tiny[:, 0:2], start=True, stop=True)\
                .then_inc(small_mm, 1)

            def add_block(k, b, bank, slot, width, a0, a1):
                if a0 == 0:
                    pe.wait_ge(sums_out, b + (NT * k + 1))
                for a in range(a0, a1):
                    for c in range(3):
                        m = nc.tensor.matmul(acc[:, bank, 0:width], A[:, slot, a, :], XS[:, a, c, 0:width],
                                             start=a == 0 and c == 0, stop=a == NT - 1 and c == 2)
                if a1 == NT:
                    m.then_inc(summed, 1)

            def make_block(b, slot, first=False):
                for j in range(PER_BLOCK):
                    pe.wait_ge(onehots, b * PER_BLOCK + (j + 2))
                    pe.wait_ge(onehots_pool, b * PER_BLOCK + (j + 2))
                    pe.wait_ge(counted, b * PER_BLOCK + (j + 1))
                    for t in range(WT):
                        h = (j % 2) * WT + t
                        m = nc.tensor.matmul(acc[:, j % 2, 0:CODES], hot_s[:, j % 2, :, t], hot_c[:, h, :],
                                             start=t == 0, stop=t == WT - 1)
                    m.then_inc(tallied, 1)
                    if not first:
                        if j == 0:
                            pe.wait_ge(counted, b * PER_BLOCK + 2)
                        add_block(0, b - 1, 3 - slot, 1 - slot, F,
                                  j * NT // PER_BLOCK, (j + 1) * NT // PER_BLOCK)

            pe.wait_ge(parts_ready, 1)
            make_block(0, 0, first=True)
            with pe.Fori(0, NT // 2) as i:
                make_block(i * 2 + 1, 1)
                make_block(i * 2 + 2, 0)
            pe.wait_ge(counted, NT * PER_BLOCK + 2)
            add_block(0, NT - 1, 2, 0, F, 0, NT)
            pe.wait_ge(weights_in, 16 * 28)

            def sums(k, width):
                pe.wait_ge(parts_ready, k + 1)

                def block(b, s):
                    pe.wait_ge(a_in[s], (b - s) * 8 + 16 * (1 + (k - 1) * ((NT + 1 - s) // 2)))
                    add_block(k, b, s, s, width, 0, NT)

                with pe.Fori(0, NT // 2) as i:
                    block(i * 2, 0)
                    block(i * 2 + 1, 1)
                block(NT - 1, 0)

            def carries(z, g):
                pe.wait_ge(z.scan_ops, SCAN0 + 4 * WIN * NIT * (g + 1))
                for h in range(2):
                    t = nc.tensor.transpose(turn[:, h, 0:P], hist[:, 1, WIN - 1, h * F:(h + 1) * F], ident[:])
                t.then_inc(z.tail_turned, 1)
                pe.wait_ge(z.carry, g + 1)
                for h in range(2):
                    t = nc.tensor.transpose(turn[:, h, P:2 * P], cin[:, h, 0:P], ident[:])
                t.then_inc(z.carry_turned, 1)

            def partials(z, l):
                if l == 0:
                    pe.sem_inc(z.part_turned, 1)
                    pe.sem_inc(z.part_product, 1)
                w = W_POST[l]
                with pe.Fori(0, NT) as b:
                    pe.wait_ge(z.rooted, b + (NT * l + 1))
                    pe.wait_ge(z.part_copied, b + (NT * l + 1))
                    for q in range(4):
                        m = nc.tensor.transpose(acc[:, 3, q * P:(q + 1) * P], operands[:, q], ident[:])
                    m.then_inc(z.part_turned, 1)
                    pe.wait_ge(z.part_copied, b + (NT * l + 2))
                    pe.wait_ge(z.partial, b + (NT * l + 1))
                    for i, (q, at) in enumerate(((0, 1), (1, 4), (1, 7), (2, 10))):
                        nc.tensor.matmul(acc[:, 2, 0:3 * F], operandsT[:, q],
                                         weights[:, w + at:w + at + 3, :].rearrange("p a f -> p (a f)"),
                                         start=i == 0, stop=False)
                    nc.tensor.matmul(acc[:, 2, 0:F], operandsT[:, 3], weights[:, w, :], start=False, stop=True)\
                        .then_inc(z.part_product, 1)

            def post(l):
                w = W_POST[l]
                bt = NT * l

                def turn_ext(b):
                    if b % GT == 0:
                        pe.wait_ge(main.ext_in[b // GT], 16 * GT * (l + 1))
                    pe.wait_ge(ext_copied, bt + b - (b % GT > 0) + PRE)
                    for h in range(2):
                        m = nc.tensor.transpose(turn[:, b % GT % 2, h * P:(h + 1) * P],
                                                EXT[:, b, h * F:(h + 1) * F], ident[:])
                    m.then_inc(ext_turned, 1)

                turn_ext(0)
                for b in range(NT + LAG):
                    if b + 1 < NT:
                        turn_ext(b + 1)
                    if b < NT:
                        pe.wait_ge(ext_copied, bt + b + 1 + PRE)
                        pe.wait_ge(lin_out, bt + b - GT + 1 + PRE)
                        for h in range(2):
                            m = nc.tensor.matmul(acc[:, b % GT, 0:3 * F],
                                                 lhs_ext[:, SLOT[b % GT], h * P:(h + 1) * P],
                                                 weights[:, w + 4 + 3 * h:w + 7 + 3 * h, :]
                                                 .rearrange("p a f -> p (a f)"), start=h == 0, stop=h == 1)
                        m.then_inc(ext_product, 1)
                    j = b - LAG
                    if j >= 0:
                        nc.tensor.matmul(acc[:, j % GT, 3 * F:4 * F], ones[0:1, :],
                                         vectors[0:1, V_BLIN[l], :], start=True, stop=False)
                        pe.wait_ge(lin_copied, bt + j + 1 + PRE)
                        nc.tensor.matmul(acc[:, j % GT, 3 * F:4 * F], lhs_u[:, SLOT[j % GT], :],
                                         weights[:, W_LIN[l], :], start=False, stop=True).then_inc(lin_product, 1)
                    j = b - LAG + 1
                    if 0 <= j < NT:
                        pe.wait_ge(u_ready, bt + j + 1)
                        pe.wait_ge(lin_copied, bt + j + PRE)
                        nc.tensor.transpose(turn_u[:, 0:P], STD[:, j, :], ident[:])\
                            .then_inc(lin_turned, 1)

            def general_sums(g):
                with pe.If(flagged(pe)):
                    carries(general, g)
                    if g > 1:
                        partials(general, g - 2)

            def dense(k, d, sources, rhs, at, gate=None):
                n = ITEMS[d]
                if gate is None:
                    pe.wait_ge(dense_in, k + 1)
                for g in range(NG):
                    for q in range(n):
                        pe.wait_ge(copied, g * n + (ITEM_BASE[d] + q))
                        if gate is not None:
                            pe.wait_ge(gate, g + 1)
                        for t in range(GT):
                            m = nc.tensor.transpose(turnf[:, t * P:(t + 1) * P],
                                                    sources[q][:, (g * GT + t) * F:(g * GT + t + 1) * F], ident[:])
                        m.then_inc(turned, 1)
                        pe.wait_ge(copied, g * n + (ITEM_BASE[d] + q + 1))
                        if q == 0:
                            pe.wait_ge(evac, g * EVAC[d] + EVAC_BASE[d])
                        c0, c1, first, final = at[q]
                        for t in range(GT):
                            m = nc.tensor.matmul(acc[:, t, c0:c1], lhs[:, q % 2, t * P:(t + 1) * P],
                                                 weights[:, rhs[q]:rhs[q] + (c1 - c0) // F, :]
                                                 .rearrange("p a f -> p (a f)"), start=first, stop=final)
                        m.then_inc(product, 1)

            flat = lambda t: t[:].rearrange("p a f -> p (a f)")
            general_sums(0)
            dense(0, "sage0", [flat(X), flat(MEAN)], [W_SAGE[0], W_SAGE[0] + 1],
                  [(0, F, True, False), (0, F, False, True)])
            sums(1, F)
            general_sums(1)
            dense(1, "sage1", [flat(H), flat(MEAN)], [W_SAGE[1], W_SAGE[1] + 1],
                  [(0, F, True, False), (0, F, False, True)])
            for l, inp in ((0, X), (1, H)):
                dense(2 + l, f"pre{l}", [flat(inp)], [W_PRE[l]], [(0, 2 * F, True, True)],
                      (x1_ready, h_ready)[l])
                sums(2 + l, 2 * F)
                partials(main, l)
                carries(main, l)
                general_sums(2 + l)
                post(l)

        @block.vector
        def _(dve):
            v = nc.vector
            chain = [0]

            link_sem = [dve_chain]

            def link(ins):
                chain[0] += 1
                ins.then_inc(link_sem[0], 1)
                dve.wait_ge(link_sem[0], chain[0])

            asks = [4]

            def ask():
                asks[0] += 1
                dve.sem_inc(act_ask, 1)
                dve.wait_ge(act_did, asks[0])

            def over_f(t):
                return t.unsqueeze(2).to_broadcast([P, NT, F])

            def over_n(i, n=NT):
                return vectors[:, i, :].unsqueeze(1).to_broadcast([P, n, F])

            link(v.memset(dstI, -1))
            link(v.memset(idx[:], 0))
            link(v.memset(X[:, NT - 1, :], 0.0))
            dve.sem_inc(padded, 1)
            dve.sem_inc(main.scan_ops, SCAN0)
            dve.sem_inc(general.scan_ops, SCAN0)
            dve.sem_inc(evac, 1)
            dve.sem_inc(windows_read, 2)
            dve.sem_inc(lin_out, PRE)
            dve.sem_inc(onehots, 1)
            link(v.memset(recpad, -1.0))
            link(v.memset(A[:, :, 0, :], 0.0))
            dve.sem_inc(zeroed, 1)
            link(v.memset(fix[:, 0, :], 0.0))
            link(v.memset(cin[:, :, 0:1], 0.0))
            dve.wait_ge(consts, 9)
            limits = tiny[:, 8:12]
            wcnt, wchunk, wstart = tiny[:, 12:16], tiny[:, 16:20], tiny[:, 20:24]
            link(v.tensor_copy(limits, limitI))
            link(v.tensor_copy(NODE, nodeI))
            link(v.tensor_copy(iota_c, jcodeI))
            link(v.tensor_copy(iota_s, jcodeI[:, 0:P].unsqueeze(2).to_broadcast([P, P, WT])))
            link(v.tensor_copy(slice_base, jsliceI))
            dve.wait_ge(dst_in, 16 * 6)
            link(v.tensor_copy(sampF, sampI))
            dve.sem_inc(pe_go, 1)
            dve.wait_ge(small_mm, 1)
            link(v.tensor_copy(samples, acc[:, 0, 0:NS]))
            link(v.tensor_scalar(LT, NODE, 0.5, None, ALU.add))
            dve.sem_inc(act_ask, 2)
            link(v.tensor_tensor(wjunk, samples.unsqueeze(1).to_broadcast([P, 4, NS]),
                                 limits.unsqueeze(2).to_broadcast([P, 4, NS]), ALU.is_lt))
            link(v.tensor_reduce(wcnt, wjunk, AX.X, ALU.add))
            link(v.tensor_scalar(wchunk, wcnt, -1.0, 0.0, ALU.add, ALU.max))
            link(v.tensor_copy(wchunkI, wchunk))
            dve.sem_inc(wchunk_ready, 1)

            def find_chunks(i):
                at = slice(BATCHES[i][0], BATCHES[i][-1] + 1)
                dve.wait_ge(act_did, i + 1)
                link(v.tensor_scalar(CHUNK[:, at], CNT[:, at], 0.5, NS / 2 - 1, ALU.mult, ALU.add))
                link(v.tensor_scalar(CHUNK[:, at], CHUNK[:, at], 0.0, None, ALU.max))
                link(v.tensor_copy(chunkI[:, at], CHUNK[:, at]))
                dve.sem_inc(chunk_ready, 1)
                dve.sem_inc(act_ask, 1)

            find_chunks(0)
            dve.wait_ge(wchunks_in, 16 * 4)
            link(v.tensor_tensor(wjunk2, wchunks, limits.unsqueeze(2).to_broadcast([P, 4, SAMPLE]), ALU.is_lt))
            link(v.tensor_reduce(wcnt, wjunk2, AX.X, ALU.add))
            link(v.scalar_tensor_tensor(wstart, wchunk, float(SAMPLE), wcnt, ALU.mult, ALU.add))
            link(v.tensor_copy(wstartI, wstart[:, 0:2]))
            dve.sem_inc(starts_ready, 1)
            link(v.tensor_tensor(wcnt[:, 0:2], wstart[:, 2:4], wstart[:, 0:2], ALU.subtract))
            link(v.tensor_tensor(wcnt[:, 0:1], wcnt[:, 0:1], wcnt[:, 1:2], ALU.max))
            link(v.tensor_scalar(wcnt[:, 0:1], wcnt[:, 0:1], float(WINDOW), None, ALU.is_gt))
            find_chunks(1)
            dve.wait_ge(src_in, 32)
            own = dstI[:, 1:STEPS + 1]
            link(v.tensor_scalar(ints1, own, SLICE - 1, None, ALU.bitwise_and))
            link(v.tensor_copy(rec[:, :, 0], ints1))
            link(v.tensor_scalar(ints1, own, SLICE.bit_length() - 1, None, ALU.arith_shift_right))
            link(v.scalar_tensor_tensor(rec[:, :, 0], ints1, float(CODES), rec[:, :, 0], ALU.mult, ALU.add))
            link(v.tensor_scalar(ints1, idx[:, 0:STEPS], P.bit_length() - 1, None, ALU.arith_shift_right))
            link(v.scalar_tensor_tensor(rec[:, :, 0], ints1, float(SLICE), rec[:, :, 0], ALU.mult, ALU.add))
            link(v.tensor_scalar(ints1, idx[:, 0:STEPS], P - 1, None, ALU.bitwise_and))
            link(v.tensor_copy(rec[:, :, 1], ints1))
            dve.sem_inc(rec_ready, 1)
            link(v.tensor_copy(dstF, dstI))
            link(v.tensor_copy(kpos, kposI))
            link(v.tensor_tensor(restart, dstF[:, 1:STEPS + 1], dstF[:, 0:STEPS], ALU.not_equal))
            link(v.tensor_tensor(ends, dstF[:, 1:STEPS + 1], dstF[:, 2:STEPS + 2], ALU.not_equal))
            fresh, inner, whole, kfirst, base = (tiny[:, i:i + 1] for i in (24, 25, 4, 26, 27))
            link(v.tensor_copy(fresh, restart[:, 0:1]))
            link(v.tensor_reduce(inner, restart[:, 1:STEPS], AX.X, ALU.add))
            link(v.memset(restart[:, 0:1], 1.0))
            link(v.tensor_scalar(neg[:], restart, -BIG, None, ALU.mult))
            link(v.tensor_scalar(inner, inner, 0.0, None, ALU.is_equal))
            link(v.tensor_scalar(tiny[:, 28:29], fresh, -1.0, 1.0, ALU.mult, ALU.add))
            link(v.tensor_tensor(whole, inner, tiny[:, 28:29], ALU.mult))
            dve.sem_inc(pe_go, 1)
            link(v.tensor_scalar(ends, ends, -OUT_OF_RANGE, OUT_OF_RANGE, ALU.mult, ALU.add))
            link(v.tensor_tensor(kpos, kpos, ends, ALU.add))
            link(v.tensor_reduce(kfirst, kpos, AX.X, ALU.min))
            link(v.tensor_scalar(base, NODE[:, 0:1], float(STEPS), None, ALU.mult))
            link(v.tensor_tensor(kfirst, kfirst, base, ALU.add))
            link(v.tensor_scalar(base, fresh, OUT_OF_RANGE, None, ALU.mult))
            link(v.tensor_tensor(kfirst, kfirst, base, ALU.add))
            link(v.tensor_copy(fixI[:], kfirst))
            dve.wait_ge(small_mm, 2)
            link(v.tensor_copy(runm[:, 0, :], acc[:, 3, 0:P]))
            link(v.tensor_scalar(runm[:, 1, :], runm[:, 0, :], BIG, -BIG, ALU.mult, ALU.add))
            link(v.tensor_scalar(runm[:, 2, :], runm[:, 0, :], -BIG, BIG, ALU.mult, ALU.add))
            dve.wait_ge(x_in, 32)

            def parts(t, at, rest):
                link(v.tensor_copy(XS[:, :, 0, at:at + F], t))
                link(v.tensor_tensor(rest, t, XS[:, :, 0, at:at + F], ALU.subtract))
                link(v.tensor_copy(XS[:, :, 1, at:at + F], rest))
                link(v.tensor_tensor(XS[:, :, 2, at:at + F], rest, XS[:, :, 1, at:at + F], ALU.subtract))

            parts(X[:], 0, C[:])
            dve.wait_ge(act_did, 4)
            link(v.tensor_scalar(CNT, CNT, 0.5, SAMPLE / 2, ALU.mult, ALU.add))
            link(v.scalar_tensor_tensor(LE, CHUNK, float(SAMPLE), CNT, ALU.mult, ALU.add))
            dve.sem_inc(pe_go, 1)
            dve.wait_ge(small_mm, 3)
            link(v.tensor_copy(LT, acc[:, 1, 0:NT]))
            link(v.tensor_tensor(M0, LE, LT, ALU.subtract))
            link(v.tensor_reduce(tiny[:, 1:2], M0, AX.X, ALU.max))
            link(v.tensor_scalar(tiny[:, 1:2], tiny[:, 1:2], float(MAX_COUNT), None, ALU.is_gt))
            link(v.tensor_tensor(tiny[:, 1:2], tiny[:, 1:2], wcnt[:, 0:1], ALU.add))
            link(v.tensor_scalar(HAS, M0, 0.0, None, ALU.is_gt))
            link(v.tensor_scalar(CNT, LE, -1.0 - P * STEPS, None, ALU.add))
            link(v.tensor_tensor(CNT, CNT, HAS, ALU.mult))
            link(v.tensor_scalar(CNT, CNT, float(P * STEPS), None, ALU.add))
            link(v.tensor_copy(endI, CNT))
            link(v.tensor_scalar(DEGC, M0, 1.0, None, ALU.max))
            link(v.reciprocal(RDEG, DEGC))
            link(v.tensor_tensor(RDEG, RDEG, HAS, ALU.mult))
            link(v.tensor_scalar(DEGC, DEGC, 1.0, None, ALU.add))
            ask()
            link(v.tensor_scalar(M0, M0, 1.0, None, ALU.add))
            ask()
            link(v.tensor_reduce(tiny[:, 0:1], LOG1, AX.X, ALU.add))
            dve.sem_inc(pe_go, 1)
            dve.wait_ge(small_mm, 4)
            avg, ravg = tiny[:, 6:7], tiny[:, 7:8]
            link(v.tensor_scalar(avg, acc[:, 2, 0:1], 1.0 / N, None, ALU.mult))
            link(v.tensor_scalar(flagI[:], acc[0:1, 2, 1:2], FLAG_FROM, None, ALU.is_ge))
            dve.sem_inc(flag_ready, 1)
            dve.sem_inc(parts_ready, 1)

            with dve.Fori(0, NT) as b:
                for j in range(PER_BLOCK):
                    dve.wait_ge(win_in[j], b * 16 + 16)
                dve.wait_ge(onehots, b * PER_BLOCK + 1)
                dve.wait_ge(onehots_pool, b * PER_BLOCK + 1)
                v.tensor_tensor(codes, win[:, :, :, 0], slice_base[:, bass.ds(b * PER_BLOCK, PER_BLOCK)]
                                .unsqueeze(2).to_broadcast([P, PER_BLOCK, WT]), ALU.subtract)\
                    .then_inc(windows_read, 1)
                v.tensor_copy(lows, win[:, :, :, 1]).then_inc(windows_read, 1)
                dve.wait_ge(windows_read, b * 2 + 4)
                for j in range(PER_BLOCK):
                    dve.wait_ge(tallied, b * PER_BLOCK + (j + 1))
                    v.tensor_tensor(hot_s[:, j % 2], iota_s,
                                    lows[:, j, :].unsqueeze(1).to_broadcast([P, P, WT]), ALU.is_equal)
                    for t in range(WT - POOL_WT):
                        m = v.tensor_scalar(hot_c[:, (j % 2) * WT + t, :], iota_c, codes[:, j, t:t + 1], None,
                                            ALU.is_equal)
                    m.then_inc(onehots, 1)
            link(v.reciprocal(ravg, avg))
            link(v.tensor_scalar(AMP, LOGD, ravg, None, ALU.mult))
            link(v.reciprocal(ATT, LOGD))
            link(v.tensor_scalar(ATT, ATT, avg, None, ALU.mult))
            dve.wait_ge(weights_in, 16 * 28)
            dve.wait_ge(sums_out, NT + 2)

            def tile(t, b):
                return t.rearrange("p a f -> p (a f)")[:, bass.ds(b * F, F)]

            def tiles(t, g):
                return t.rearrange("p a f -> p (a f)")[:, bass.ds(g * (GT * F), GT * F)]\
                    .rearrange("p (a f) -> p a f", f=F)

            def front(z, l, b):
                dve.wait_ge(z.means, b + (NT * l + 1))
                v.tensor_tensor(operands[:, 0], operands[:, 0], operands[:, 1], ALU.add)
                v.scalar_tensor_tensor(operands[:, 2], tile(STD, b), RDEG[:, bass.ds(b, 1)], operands[:, 2],
                                       ALU.mult, ALU.subtract).then_inc(z.varied, 1)
                dve.wait_ge(z.varied, b * 2 + (NT * 2 * l + 1))
                v.tensor_scalar(operands[:, 2], operands[:, 2], 0.0, EPS, ALU.max, ALU.add).then_inc(z.varied, 1)

            def combine(u, bank, b, add, step):
                step(v.tensor_tensor(u, acc[:, bank, 0:F], add, ALU.add))
                step(v.scalar_tensor_tensor(u, acc[:, bank, F:2 * F], AMP[:, bass.ds(b, 1)], u,
                                            ALU.mult, ALU.add))
                step(v.scalar_tensor_tensor(u, acc[:, bank, 2 * F:3 * F], ATT[:, bass.ds(b, 1)], u,
                                            ALU.mult, ALU.add))

            def take_apart(t, rest, g, at, step):
                p0, p1, p2 = (XS.rearrange("p a c f -> p (a c f)")[:, bass.ds(g * (GT * 6 * F), GT * 6 * F)]
                              .rearrange("p (a c f) -> p a c f", c=3, f=2 * F)[:, :, c, at:at + F]
                              for c in range(3))
                step(v.tensor_copy(p0, t))
                step(v.tensor_tensor(rest, t, p0, ALU.subtract))
                step(v.tensor_copy(p1, rest))
                step(v.tensor_tensor(p2, rest, p1, ALU.subtract))

            def group_parts(l, g, squared):
                n = [0]

                def step(ins):
                    n[0] += 1
                    ins.then_inc(parts_chain, 1)
                    dve.wait_ge(parts_chain, g * 9 + (9 * NG * l + 5 * squared + n[0]))

                t = tiles(STD if squared else Y[:], g)
                if not squared:
                    step(v.tensor_tensor(tiles(STD, g), t, t, ALU.mult))
                take_apart(t, tiles(MEAN, g), g, squared * F, step)

            def back(z, l, b):
                dve.wait_ge(z.part_product, b + (NT * l + 2))
                n = [0]

                def step(ins):
                    n[0] += 1
                    ins.then_inc(z.combined, 1)
                    dve.wait_ge(z.combined, b * 3 + (NT * 3 * l + n[0]))

                combine(tile(STD, b), 2, b, vectors[:, V_BPOST[l], :], step)
                dve.sem_inc(z.partial, 1)

            def open_scan(z):
                link(v.memset(hist[:, 1, WIN - 1, :], 0.0))
                for w in range(2):
                    link(v.tensor_copy(stage[:, w, :], idx[:, w * WIN:(w + 1) * WIN]))
                dve.sem_inc(z.staged, 2)
                dve.sem_inc(z.start, 1)

            def scan(z, g, kind):
                col = keep if kind == SUM else neg
                o0, o0b = (ALU.mult, ALU.mult) if kind == SUM else (ALU.add, ALU.subtract)
                o1, o2 = (ALU.add, ALU.add) if kind == SUM else (ALU.max, ALU.min)
                def windows(it, fronts=(None, None), backs=(None, None), group=None):
                    for w in range(2):
                        dve.wait_ge(z.landed[w], it * (16 * WIN) + 16 * WIN * (NIT * g + 1))
                        if kind == SUM:
                            dve.wait_ge(z.squared, it * 2 + (2 * NIT * g + w + 1))
                        dve.wait_ge(z.stored[w], it * 32 + 16 * (1 + 2 * NIT * g))
                        for s in range(WIN):
                            done = it * (4 * WIN) + (SCAN0 + 4 * WIN * NIT * g + 2 * WIN * w + 2 * s - 1)
                            last = hist[:, w, s - 1, :] if s else hist[:, 1 - w, WIN - 1, :]
                            k = (it * 2 + w) * WIN + s
                            second = squares if kind == SUM else rows
                            dve.wait_ge(z.scan_ops, done)
                            v.scalar_tensor_tensor(hist[:, w, s, 0:F], last[:, 0:F], col[:, bass.ds(k, 1)],
                                                   rows[:, w, s, :], o0, o1).then_inc(z.scan_ops, 1)
                            dve.wait_ge(z.scan_ops, done + 1)
                            v.scalar_tensor_tensor(hist[:, w, s, F:2 * F], last[:, F:2 * F],
                                                   col[:, bass.ds(k, 1)], second[:, w, s, :], o0b, o2)\
                                .then_inc(z.scan_ops, 1)
                        v.tensor_copy(stage[:, w, :], idx[:, bass.ds((it * 2 + w + 2) * WIN, WIN)])\
                            .then_inc(z.staged, 1)
                        if group is not None:
                            group_parts(g, group, w)
                        if backs[w] is not None:
                            back(z, g, backs[w])
                        if fronts[w] is not None:
                            front(z, g, fronts[w])

                if kind == SUM:
                    with dve.Fori(0, NIT) as it:
                        windows(it)
                else:
                    half = NIT // 2
                    with dve.Fori(0, NG) as it:
                        windows(it, group=it)
                    dve.sem_inc(parts_ready, 1)
                    with dve.Fori(NG, half) as it:
                        windows(it)
                    windows(half, (0, 1), (None, 0))
                    with dve.Fori(half + 1, half + NT // 2) as it:
                        windows(it, ((it - half) * 2, (it - half) * 2 + 1), ((it - half) * 2 - 1, (it - half) * 2))
                    windows(half + NT // 2, (NT - 1, None), (NT - 2, NT - 1))
                    for it in range(half + NT // 2 + 1, NIT):
                        windows(it)
                dve.wait_ge(z.tail_turned, g + 1)
                for h, op in ((0, o1), (1, o2)):
                    m = 0 if kind == SUM else 1 + h
                    link(v.tensor_tensor_scan(cin[:, h, 1:P + 1], runm[:, m, :], turn[:, h, 0:P], 0.0,
                                              o0, op))
                dve.sem_inc(z.carry, 1)
                dve.wait_ge(z.carry_turned, g + 1)
                dve.wait_ge(z.first_in, 16 * (g + 1))
                for h, op in ((0, o1), (1, o2)):
                    link(v.tensor_tensor(fix[:, 1, h * F:(h + 1) * F], fix[:, 0, h * F:(h + 1) * F],
                                         turn[:, h, P:2 * P], op))
                dve.sem_inc(z.fixed, 1)

            link_base = [0]

            def general_sums(g):
                before = chain[0]
                chain[0] = 0
                link_sem[0] = general_chain[g]
                with dve.If(flagged(dve)):
                    if g > 1:
                        for i in range(NG):
                            dve.wait_ge(main.ext_in[i], 16 * GT * (g - 1))
                        dve.sem_inc(spill_ready, 1)
                        dve.wait_ge(spilled, 16 * (2 * (g - 2) + 1))
                    for w in range(2):
                        dve.wait_ge(a_stored[w], 16 * (1 + (NT + 1 - w) // 2))
                    link(v.tensor_scalar(keep, neg[:], 0.0, None, ALU.is_equal))
                    open_scan(general)
                    scan(general, g, SUM)
                    for i in range(NG):
                        dve.wait_ge(general.ext_in[i], 16 * GT * (g + 1))
                    link(v.tensor_copy(MEAN, EXT[:, :, 0:F]))
                    link(v.tensor_copy(STD, EXT[:, :, F:2 * F]))
                    if g < 2:
                        link(v.tensor_tensor(MEAN, MEAN, over_f(RDEG), ALU.mult))
                    if g > 1:
                        dve.sem_inc(unspill_ready, 1)
                        dve.wait_ge(spilled, 16 * (2 * (g - 2) + 2))
                        if g == 2:
                            dve.sem_inc(general.partial, 1)
                        dve.sem_inc(general.sums_in, 1)
                        with dve.Fori(0, NT) as b:
                            front(general, g - 2, b)
                            back(general, g - 2, b)
                chain[0] = before
                link_sem[0] = dve_chain

            def evacuate(d, step):
                n, m = ITEMS[d], EVAC[d]
                if d == "sage0":
                    dve.sem_inc(dense_in, 1)
                with dve.Fori(0, NG) as g:
                    dve.wait_ge(product, g * n + (ITEM_BASE[d] + n))
                    step(g)
                dve.wait_ge(evac, EVAC_BASE[d] + NG * m)

            counted = [0]

            def moments_of_group(mark, need):
                for t in range(GT):
                    mark(v.bn_stats(bn[:, GT + t, :], staged[:, t, :]))
                need()
                dve.sem_inc(bn_ready, 1)
                for t in range(GT):
                    mark(v.bn_aggr(stats[:, 1, t, :], bn[:, GT + t, :]))

            def ordered(order, g, per, start):
                counted[0] = 0

                def mark(ins):
                    counted[0] += 1
                    ins.then_inc(order, 1)
                    return counted[0]

                def need(k=None):
                    dve.wait_ge(order, g * per + (start + (counted[0] if k is None else k)))
                return mark, need

            def ask_root(second, mark, need):
                need()
                mark(v.tensor_scalar(M1[:, 0:GT], stats[:, second, :, 1], EPS, None, ALU.add))
                need()
                dve.sem_inc(root_ask, 1)

            def normalise(dest, second, asked, mark, need):
                dve.wait_ge(root_did, asked + 1)
                mark(v.reciprocal(rstd, M2[:, 0:GT]))
                need()
                for t in range(GT):
                    mark(v.tensor_scalar(dest[:, t, :], staged[:, t, :], stats[:, second, t, 0:1],
                                         rstd[:, t:t + 1], ALU.subtract, ALU.mult))
                need()

            general_sums(0)

            def hidden(g):
                n = [0]

                def step(ins):
                    n[0] += 1
                    ins.then_inc(hidden_chain, 1)
                    dve.wait_ge(hidden_chain, g * 6 + n[0])

                h = tiles(H[:], g)
                step(v.tensor_tensor(h, acc[:, :, 0:F], over_n(V_B[0], GT), ALU.add))
                dve.sem_inc(evac, 1)
                step(v.tensor_scalar(h, h, 0.0, None, ALU.max))
                take_apart(h, tiles(Y[:], g), g, 0, step)

            evacuate("sage0", hidden)
            dve.sem_inc(table_ready, 1)
            dve.sem_inc(parts_ready, 1)
            dve.wait_ge(sums_out, 2 * NT + 2)
            general_sums(1)

            def result(g, mark, need, first=False):
                dve.wait_ge(product, g * ITEMS["sage1"] + (ITEM_BASE["sage1"] + ITEMS["sage1"]))
                y = tiles(Y[:], g)
                mark(v.tensor_tensor(y, acc[:, :, 0:F], over_n(V_B[1], GT), ALU.add))
                need()
                dve.sem_inc(evac, 1)
                if not first:
                    scaled(g - 1, mark, need)
                mark(v.tensor_tensor(staged, y, tiles(X[:], g), ALU.add))
                need()
                moments_of_group(mark, need)
                ask_root(1, mark, need)

            def scaled(g, mark, need):
                normalise(tiles(X[:], g), 1, g, mark, need)
                dve.sem_inc(x1_ready, 1)

            dve.sem_inc(dense_in, 1)
            result(0, *ordered(result_chain, 0, 0, 0), first=True)
            opening, per = counted[0], counted[0] + 1 + GT
            with dve.Fori(1, NG) as g:
                result(g, *ordered(result_chain, g, per, opening - per))
                assert counted[0] == per
            scaled(NG - 1, *ordered(result_chain, 0, 0, opening + per * (NG - 1)))

            def post(l):
                bt = NT * l
                n = counted

                def body(g, per, start):
                    return ordered(post_chain[l], g, per, start)

                def tile_step(b, t, j, mark, need):
                    if b is not None:
                        u = tile(STD, b)
                        dve.wait_ge(ext_product, b + (bt + 1 + PRE))
                        u1 = mark(v.tensor_tensor(u, acc[:, t, 0:F], u, ALU.add))
                    if j is not None:
                        bank = (t - OUT_LAG) % GT
                        dve.wait_ge(lin_product, j + (bt + 1 + PRE))
                        mark(v.tensor_copy(tile(Y[:], j), acc[:, bank, 3 * F:4 * F]))
                    if b is not None:
                        need(u1)
                        u2 = mark(v.scalar_tensor_tensor(u, acc[:, t, F:2 * F], AMP[:, bass.ds(b, 1)], u,
                                                         ALU.mult, ALU.add))
                    if j is not None:
                        z2 = mark(v.bn_stats(bn[:, bank, :], acc[:, bank, 3 * F:4 * F]))
                    if b is not None:
                        need(u2)
                        v.scalar_tensor_tensor(u, acc[:, t, 2 * F:3 * F], ATT[:, bass.ds(b, 1)], u,
                                               ALU.mult, ALU.add).then_inc(u_ready, 1)
                    if j is not None:
                        need(z2)
                        dve.sem_inc(lin_out, 1)
                        mark(v.bn_aggr(stats[:, 0, bank, :], bn[:, bank, :]))

                def ask_first(mark, need):
                    need()
                    mark(v.tensor_scalar(negmean, stats[:, 0, :, 0], -1.0, None, ALU.mult))
                    ask_root(0, mark, need)

                def scale_group(asked, mark, need):
                    dve.wait_ge(root_did, asked + 1)
                    mark(v.reciprocal(scales, M2[:, 0:GT]))
                    need()
                    mark(v.tensor_tensor(shifts, negmean, scales, ALU.mult))
                    need()
                    dve.sem_inc(scales_ready, 1)

                def weight(g0, mark, need):
                    dve.wait_ge(normed, g0 * GT + (NT * l + GT))
                    y = tiles(Y[:], g0)
                    mark(v.tensor_tensor(y, y, over_n(V_LNW[l], GT), ALU.mult))
                    need()

                def bias(g0, mark, need):
                    y = tiles(Y[:], g0)
                    mark(v.tensor_tensor(y, y, over_n(V_LNB[l], GT), ALU.add))
                    need()

                def residual(g0, mark, need):
                    y = tiles(Y[:], g0)
                    if l == 0:
                        mark(v.scalar_tensor_tensor(tiles(H[:], g0), y, 0.0, tiles(X[:], g0), ALU.max, ALU.add))
                        need()
                        dve.sem_inc(h_ready, 1)
                    else:
                        mark(v.tensor_tensor(staged, y, tiles(X[:], g0), ALU.add))
                        need()
                        moments_of_group(mark, need)
                        ask_root(1, mark, need)

                def result(g0, asked, mark, need):
                    normalise(tiles(Y[:], g0), 1, asked, mark, need)
                    dve.sem_inc(out_ready, 1)

                def group(g, mark, need, prev, prev2, tiles_left=True):
                    for t in range(GT):
                        out = (t >= OUT_LAG or prev) if tiles_left else t < OUT_LAG
                        tile_step(g * GT + t if tiles_left else None, t,
                                  g * GT + (t - OUT_LAG) if out else None, mark, need)
                        if t == 1 and prev2:
                            weight(g - 2, mark, need)
                        if t == 2 and prev2:
                            bias(g - 2, mark, need)
                        if t == OUT_LAG - 1 and prev:
                            ask_first(mark, need)
                        if t == OUT_LAG and prev:
                            scale_group(first_root(l, g - 1, prev2), mark, need)
                        if t == OUT_LAG and prev2:
                            residual(g - 2, mark, need)
                        if t == OUT_LAG + 1 and prev2 and l == 1:
                            result(g - 2, second_root(g - 2), mark, need)

                group(0, *body(0, 0, 0), False, False)
                opening = counted[0]
                group(1, *body(1, 0, opening), True, False)
                opening += counted[0]
                per = GT * 5 + 4 + 3 + l * (2 * GT + 1 + 1 + GT)
                with dve.Fori(2, NG) as g:
                    group(g, *body(g, per, opening - 2 * per), True, True)
                    assert counted[0] == per
                opening += per * (NG - 2)
                group(NG, *body(0, 0, opening), True, True, tiles_left=False)
                opening += counted[0]
                mark, need = body(0, 0, opening)
                weight(NG - 1, mark, need)
                bias(NG - 1, mark, need)
                residual(NG - 1, mark, need)
                if l == 1:
                    result(NG - 1, second_root(NG - 1) - 1, mark, need)

            dve.sem_inc(main.partial, 1)
            for l, inp in ((0, X), (1, H)):
                d = f"pre{l}"

                def split(g):
                    v.tensor_tensor(tiles(C[:], g), acc[:, :, 0:F], over_n(V_BPRE[l], GT), ALU.add)\
                        .then_inc(evac, 1)
                    v.tensor_copy(tiles(Y[:], g), acc[:, :, F:2 * F]).then_inc(evac, 1)
                    dve.wait_ge(evac, g * EVAC[d] + (EVAC_BASE[d] + EVAC[d]))
                    dve.sem_inc(rows_ready, 1)

                evacuate(d, split)
                open_scan(main)
                scan(main, l, EXTREME)

                if l == 1:
                    link(v.tensor_tensor(X[:], X[:], H[:], ALU.add))
                general_sums(2 + l)
                post(l)


_INS = ['x', 'src', 'dst', 'L0_gnn_W_self1', 'L0_gnn_W_neigh1', 'L0_gnn_b1', 'L0_gnn_W_self2', 'L0_gnn_W_neigh2',
        'L0_gnn_b2', 'L1_gnn_W_pre0', 'L1_gnn_b_pre0', 'L1_gnn_W_post0', 'L1_gnn_b_post0', 'L1_gnn_W_lin0',
        'L1_gnn_b_lin0', 'L1_gnn_ln_w0', 'L1_gnn_ln_b0', 'L1_gnn_W_pre1', 'L1_gnn_b_pre1', 'L1_gnn_W_post1',
        'L1_gnn_b_post1', 'L1_gnn_W_lin1', 'L1_gnn_b_lin1', 'L1_gnn_ln_w1', 'L1_gnn_ln_b1']


def kernel(**inputs):
    import numpy as np
    import concourse.bacc as bacc
    from concourse.bass_utils import run_bass_kernel_spmd

    nc = bacc.Bacc("TRN2", target_bir_lowering=False, num_devices=1)
    arrays, args = {}, []
    for name in _INS:
        a = np.ascontiguousarray(inputs[name])
        arrays[f"in_{name}"] = a
        args.append(nc.dram_tensor(f"in_{name}", a.shape, mybir.dt.from_np(a.dtype), kind="ExternalInput").ap())
    out = nc.dram_tensor("out", (N, F), F32, kind="ExternalOutput").ap()
    gnn_kernel(nc, *args, out)
    return run_bass_kernel_spmd(nc, [arrays], core_ids=[0]).results[0]["out"]
```
